# Optimizing a Trainium2 kernel written in Bass

```python
import numpy as np
import jax
import jax.numpy as jnp

def _softmax(x, axis=-1):
    return jax.nn.softmax(x, axis=axis)

def _gelu(x):
    return jax.nn.gelu(x, approximate=True)

def _silu(x):
    return jax.nn.silu(x)

def _sigmoid(x):
    return jax.nn.sigmoid(x)

def _layernorm(x, axis=-1, eps=1e-05):
    m = jnp.mean(x, axis=axis, keepdims=True)
    v = jnp.var(x, axis=axis, keepdims=True)
    return (x - m) / jnp.sqrt(v + eps)

def _scatter_add(tgt, idx, src, axis=0):
    return tgt.at[idx].add(src)

def _segment_sum(src, seg, n):
    return jax.ops.segment_sum(src, seg, n)
kernel_name = 'mk_prb_d1_jaxref_r4_9d404d'

def setup_inputs(seed: int=0):
    np.random.seed(seed)
    _w = jnp.asarray

    def _L0_attn_setup():
        import jax, jax.numpy as jnp
        import numpy as np
        B, S, HID = (1, 512, 1024)
        NH, NKV = (32, 8)
        HD = HID // NH
        GROUPS = NH // NKV
        ROPE_THETA = 10000.0

        def _rope_cos_sin(seq_len, head_dim, dtype=jnp.float32):
            inv_freq = 1.0 / ROPE_THETA ** (jnp.arange(0, head_dim, 2, dtype=jnp.float32) / head_dim)
            t = jnp.arange(seq_len, dtype=jnp.float32)
            freqs = jnp.outer(t, inv_freq)
            emb = jnp.concatenate([freqs, freqs], axis=-1)
            return (jnp.cos(emb).astype(dtype), jnp.sin(emb).astype(dtype))

        def _rotate_half(x):
            x1, x2 = jnp.split(x, 2, axis=-1)
            return jnp.concatenate([-x2, x1], axis=-1)

        def _apply_rope(x, cos, sin):
            return x * cos[None, None] + _rotate_half(x) * sin[None, None]
        key = jax.random.key(seed)
        k1, k2, k3, k4, k5 = jax.random.split(key, 5)
        return {'hidden_states': jax.random.normal(k1, (B, S, HID), jnp.float32), 'Wq': jax.random.normal(k2, (NH * HD, HID), jnp.float32) * 0.02, 'Wk': jax.random.normal(k3, (NKV * HD, HID), jnp.float32) * 0.02, 'Wv': jax.random.normal(k4, (NKV * HD, HID), jnp.float32) * 0.02, 'Wo': jax.random.normal(k5, (HID, NH * HD), jnp.float32) * 0.02}
    _L0_attn_in = _L0_attn_setup()

    def _L0_ffn_setup():
        import jax, jax.numpy as jnp
        import numpy as np
        B, S, D, O, E, R = (2, 1024, 1024, 1024, 8, 16)
        TOP_K = 2
        SCALING = 32.0 / 16.0
        key = jax.random.key(seed)
        k = jax.random.split(key, 6)
        x = jax.random.normal(k[0], (B, S, D), dtype=jnp.float32)
        W_base = jax.random.normal(k[1], (O, D), dtype=jnp.float32) * 0.02
        b_base = jax.random.normal(k[2], (O,), dtype=jnp.float32) * 0.02
        W_router = jax.random.normal(k[3], (E, D), dtype=jnp.float32) * 0.01
        lora_A = jax.random.normal(k[4], (E, R, D), dtype=jnp.float32) * (1.0 / np.sqrt(D))
        lora_B = jax.random.normal(k[5], (E, O, R), dtype=jnp.float32) * 0.02
        return {'x': x, 'W_base': W_base, 'b_base': b_base, 'W_router': W_router, 'lora_A': lora_A, 'lora_B': lora_B}
    _L0_ffn_in = _L0_ffn_setup()
    _d = {'L0_attn_hidden_states': _L0_attn_in['hidden_states'], 'L0_attn_Wq': _L0_attn_in['Wq'], 'L0_attn_Wk': _L0_attn_in['Wk'], 'L0_attn_Wv': _L0_attn_in['Wv'], 'L0_attn_Wo': _L0_attn_in['Wo'], 'L0_ffn_W_base': _L0_ffn_in['W_base'], 'L0_ffn_b_base': _L0_ffn_in['b_base'], 'L0_ffn_W_router': _L0_ffn_in['W_router'], 'L0_ffn_lora_A': _L0_ffn_in['lora_A'], 'L0_ffn_lora_B': _L0_ffn_in['lora_B']}
    _x0 = _d['L0_attn_hidden_states']
    _d['L0_attn_hidden_states'] = jax.random.normal(jax.random.fold_in(jax.random.key(seed), 1), (2, 2048, 1024), dtype=_x0.dtype)
    del _x0
    return _d

def reference(L0_attn_hidden_states, L0_attn_Wq, L0_attn_Wk, L0_attn_Wv, L0_attn_Wo, L0_ffn_W_base, L0_ffn_b_base, L0_ffn_W_router, L0_ffn_lora_A, L0_ffn_lora_B):

    def _L0_attn_ref(hidden_states, Wq, Wk, Wv, Wo):
        import jax, jax.numpy as jnp
        import numpy as np
        B, S, HID = (1, 512, 1024)
        NH, NKV = (32, 8)
        HD = HID // NH
        GROUPS = NH // NKV
        ROPE_THETA = 10000.0

        def _rope_cos_sin(seq_len, head_dim, dtype=jnp.float32):
            inv_freq = 1.0 / ROPE_THETA ** (jnp.arange(0, head_dim, 2, dtype=jnp.float32) / head_dim)
            t = jnp.arange(seq_len, dtype=jnp.float32)
            freqs = jnp.outer(t, inv_freq)
            emb = jnp.concatenate([freqs, freqs], axis=-1)
            return (jnp.cos(emb).astype(dtype), jnp.sin(emb).astype(dtype))

        def _rotate_half(x):
            x1, x2 = jnp.split(x, 2, axis=-1)
            return jnp.concatenate([-x2, x1], axis=-1)

        def _apply_rope(x, cos, sin):
            return x * cos[None, None] + _rotate_half(x) * sin[None, None]
        bsz, q_len, _ = hidden_states.shape
        q = (hidden_states @ Wq.T).reshape(bsz, q_len, NH, HD).transpose(0, 2, 1, 3)
        k = (hidden_states @ Wk.T).reshape(bsz, q_len, NKV, HD).transpose(0, 2, 1, 3)
        v = (hidden_states @ Wv.T).reshape(bsz, q_len, NKV, HD).transpose(0, 2, 1, 3)
        cos, sin = _rope_cos_sin(q_len, HD, hidden_states.dtype)
        q = _apply_rope(q, cos, sin)
        k = _apply_rope(k, cos, sin)
        k = jnp.repeat(k, GROUPS, axis=1)
        v = jnp.repeat(v, GROUPS, axis=1)
        scale = 1.0 / jnp.sqrt(jnp.asarray(HD, hidden_states.dtype))
        logits = jnp.einsum('bhqd,bhkd->bhqk', q, k) * scale
        causal = jnp.tril(jnp.ones((q_len, q_len), dtype=bool))
        logits = jnp.where(causal[None, None], logits, jnp.finfo(logits.dtype).min)
        attn = jax.nn.softmax(logits, axis=-1)
        out = jnp.einsum('bhqk,bhkd->bhqd', attn, v)
        out = out.transpose(0, 2, 1, 3).reshape(bsz, q_len, NH * HD)
        return out @ Wo.T

    def _L0_ffn_ref(x, W_base, b_base, W_router, lora_A, lora_B):
        import jax, jax.numpy as jnp
        import numpy as np
        B, S, D, O, E, R = (2, 1024, 1024, 1024, 8, 16)
        TOP_K = 2
        SCALING = 32.0 / 16.0
        d = x.shape[-1]
        n_experts = W_router.shape[0]
        xf = x.reshape(-1, d)
        logits = xf @ W_router.T
        probs = jax.nn.softmax(logits, axis=-1)
        topk_p, topk_i = jax.lax.top_k(probs, TOP_K)
        topk_p = topk_p / jnp.sum(topk_p, axis=-1, keepdims=True)
        w = jnp.sum(jax.nn.one_hot(topk_i, n_experts, dtype=xf.dtype) * topk_p[..., None], axis=1)
        h = jnp.einsum('td,erd->ter', xf, lora_A)
        lora_out = jnp.einsum('ter,eor,te->to', h, lora_B, w) * SCALING
        base = x @ W_base.T + b_base
        return base + lora_out.reshape(x.shape[:-1] + (W_base.shape[0],))
    x = L0_attn_hidden_states
    xn = _layernorm(x, axis=-1)
    x = x + _L0_attn_ref(xn, L0_attn_Wq, L0_attn_Wk, L0_attn_Wv, L0_attn_Wo) + _L0_ffn_ref(xn, L0_ffn_W_base, L0_ffn_b_base, L0_ffn_W_router, L0_ffn_lora_A, L0_ffn_lora_B)
    return x

_drawn_inputs = setup_inputs


def setup_inputs(seed=0):
    import zlib

    import numpy as np

    out = dict(_drawn_inputs(seed))
    spreads = {}
    factors = {'L0_attn_Wq': 5.396, 'L0_attn_Wk': 4.622, 'L0_ffn_b_base': 3.438}
    for name, (base, spread) in spreads.items():
        noise = np.random.default_rng([zlib.crc32(name.encode()), seed]).standard_normal(out[name].shape)
        drawn = base * np.exp(spread * noise) if base else spread * noise
        out[name] = jnp.asarray(drawn.astype(out[name].dtype))
    for name, factor in factors.items():
        out[name] = (out[name] * factor).astype(out[name].dtype)
    return out
```

```python
from contextlib import ExitStack

import concourse.bass as bass
from concourse import mybir

F32 = mybir.dt.float32
F32R = mybir.dt.float32r
BF16 = mybir.dt.bfloat16
U32 = mybir.dt.uint32
ALU = mybir.AluOpType
ACT = mybir.ActivationFunctionType
AX = mybir.AxisListType

P = 128
BATCH, SEQ, HID = 2, 2048, 1024
NH, NKV, HD = 32, 8, 32
GQ = NH // NKV
HALF = HD // 2
EXPERTS, RANK = 8, 16
TOKENS = BATCH * SEQ
TILES = TOKENS // P
KT = HID // P
KVW = NKV * HD
QKVW = HID + 2 * KVW
BANK = 512
QKH = NH + NKV
FT = QKH * HD // P
GROUPS = BATCH * NKV
CH = SEQ // BANK
KTILES = SEQ // P
PER = BANK // P
EPS = 1e-5
SM_SCALE = float(HD) ** -0.5
LORA_SCALE = 2.0
MROW = 3 * HD
KROWS = MROW + 2
ADW = EXPERTS * RANK
ARW = ADW + EXPERTS


class Scope:

    def __init__(self, nc, ctx, tag):
        self.nc, self.ctx, self.tag = nc, ctx, tag

    def sb(self, name, shape, dtype):
        return self.ctx.enter_context(self.nc.sbuf_tensor(f"{self.tag}_{name}", shape, dtype))

    def ps(self, name, shape, dtype=F32):
        return self.ctx.enter_context(self.nc.psum_tensor(f"{self.tag}_{name}", shape, dtype))

    def sem(self, name):
        return self.ctx.enter_context(self.nc.semaphore(f"{self.tag}_{name}"))


def by_pairs(eng, count, tile):
    tile(0, 0)
    tile(1, 1)
    with eng.Fori(1, count // 2 - 1) as i:
        tile(2 * i, 0)
        tile(2 * i + 1, 1)
    tile(count - 2, 0)
    tile(count - 1, 1)


def before(n, k):
    return isinstance(n, int) and n < k


def wait_alone(eng, sem, value, waited):
    eng.wait_ge(sem, value)
    eng.sem_inc(waited, 1)


def three_passes(pe, out, sta_hi, sta_lo, mov_hi, mov_lo, first, last):
    pe.matmul(out, sta_hi, mov_hi, start=first, stop=False)
    pe.matmul(out, sta_hi, mov_lo, start=False, stop=False)
    return pe.matmul(out, sta_lo, mov_hi, start=False, stop=last)


def project_qkv(nc, x, wq, wk, wv, rope, ident_d, q_s, k_s, v_s):
    with ExitStack() as ctx:
        s = Scope(nc, ctx, "p1")
        ident = s.sb("ident", [P, P], F32)
        w_nat = s.sb("w_nat", [P, 2, HID], F32)
        w_hi = s.sb("w_hi", [P, KT, QKVW], F32R)
        w_lo = s.sb("w_lo", [P, KT, QKVW], F32R)
        x_t = s.sb("x", [P, 2, HID], F32)
        rope_t = s.sb("rope", [P, 2, 2 * HD], F32)
        bn = s.sb("bn", [P, 2, HID // BANK, 6], F32)
        mean_var = s.sb("mean_var", [P, 2, 2], F32)
        var_eps = s.sb("var_eps", [P, 2], F32)
        rstd = s.sb("rstd", [P, 2], F32)
        minus_half = s.sb("minus_half", [P, 1], F32)
        xt_hi = s.sb("xt_hi", [P, 2, KT, P], F32R)
        xt_lo = s.sb("xt_lo", [P, 2, KT, P], F32R)
        by_cos = s.sb("by_cos", [P, QKH, HD], F32)
        by_sin = s.sb("by_sin", [P, QKH, HD], F32)
        rot = s.sb("rot", [P, QKH * HD], F32)
        v_t = s.sb("v", [P, 2, KVW], F32)
        f_hi = s.sb("f_hi", [P, FT, P], F32R)
        f_lo = s.sb("f_lo", [P, FT, P], F32R)
        tp = s.ps("tp", [P, KT * P])
        qkv = s.ps("qkv", [P, QKVW])
        ft = s.ps("ft", [P, 3 * BANK])

        consts_in = s.sem("consts_in")
        waited = s.sem("waited")
        w_in = [s.sem("w_in0"), s.sem("w_in1")]
        w_tp = s.sem("w_tp")
        w_hi_ok = s.sem("w_hi_ok")
        w_lo_ok = s.sem("w_lo_ok")
        x_in = [s.sem("x_in0"), s.sem("x_in1")]
        bn_ok = s.sem("bn_ok")
        agg_ok = s.sem("agg_ok")
        eps_ok = s.sem("eps_ok")
        rstd_ok = s.sem("rstd_ok")
        xn_ok = s.sem("xn_ok")
        tp_ok = s.sem("tp_ok")
        xh_ok = s.sem("xh_ok")
        xl_ok = s.sem("xl_ok")
        mm_ok = s.sem("mm_ok")
        cs_ok = s.sem("cs_ok")
        v_ok = s.sem("v_ok")
        rot_ok = s.sem("rot_ok")
        ft_ok = s.sem("ft_ok")
        fh_ok = s.sem("fh_ok")
        fl_ok = s.sem("fl_ok")
        f_out = s.sem("f_out")
        v_out = [s.sem("v_out0"), s.sem("v_out1")]
        mh_ok = s.sem("mh_ok")

        weights = [(wq, r, r * P) for r in range(HID // P)]
        weights += [(wk, r, HID + r * P) for r in range(KVW // P)]
        weights += [(wv, r, HID + KVW + r * P) for r in range(KVW // P)]
        NW = len(weights)
        BANKS = QKVW // BANK
        heads_in = [(c * BANK // HD, min((c + 1) * BANK // HD, QKH)) for c in range(BANKS)]

        block = ctx.enter_context(nc.Block())

        @block.sync
        def _(sp):
            sp.dma_start(ident[:], ident_d).then_inc(consts_in, 16)
            for n, (w, r, _) in enumerate(weights):
                if n >= 2:
                    sp.wait_ge(w_tp, n - 1)
                sp.dma_start(w_nat[:, n % 2, :], w[r * P:(r + 1) * P, :]).then_inc(w_in[n % 2], 16)

            def load(n, u):
                if not before(n, 2):
                    wait_alone(sp, tp_ok, n - 1, waited)
                    sp.wait_ge(cs_ok, BANKS * (n - 1))
                sp.dma_start(x_t[:, u, :], x[bass.ds(n * P, P), :]).then_inc(x_in[u], 16)
                sp.dma_start(rope_t[:, u, :], rope[bass.ds(n * P, P), :]).then_inc(x_in[u], 16)

            def store(n, u):
                toks = bass.ds(n * P, P)
                wait_alone(sp, v_ok, n + 1, waited)
                sp.dma_start(v_s[toks, :], v_t[:, u, :]).then_inc(v_out[u], 16)
                for half, f, ready in ((0, f_hi, fh_ok), (1, f_lo, fl_ok)):
                    wait_alone(sp, ready, n + 1, waited)
                    sp.dma_start(q_s[half, :, toks].rearrange("(f p) t -> p f t", p=P),
                                 f[:, 0:HID // P, :].bitcast(F32)).then_inc(f_out, 16)
                    sp.dma_start(k_s[half, :, toks].rearrange("(f p) t -> p f t", p=P),
                                 f[:, HID // P:FT, :].bitcast(F32)).then_inc(f_out, 16)

            load(0, 0)
            load(1, 1)
            by_pairs(sp, TILES - 2, lambda n, u: (load(n + 2, u), store(n, u)))
            store(TILES - 2, 0)
            store(TILES - 1, 1)
            sp.wait_ge(f_out, 64 * TILES)
            for u in range(2):
                sp.wait_ge(v_out[u], 16 * TILES // 2)

        @block.gpsimd
        def _(pool):
            pool.memset(minus_half[:], -0.5).then_inc(mh_ok, 1)
            pool.wait_ge(mh_ok, 1)

            def rstd_of(n, u):
                wait_alone(pool, agg_ok, n + 1, waited)
                pool.tensor_scalar(var_eps[:, u:u + 1], mean_var[:, u, 1:2], EPS, None, ALU.add).then_inc(eps_ok, 1)
                pool.wait_ge(eps_ok, n + 1)
                pool.tensor_tensor(rstd[:, u:u + 1], var_eps[:, u:u + 1], minus_half[:], ALU.pow).then_inc(rstd_ok, 1)

            def rotate(n, u):
                pool.wait_ge(cs_ok, BANKS * (n + 1))
                if not before(n, 1):
                    pool.wait_ge(ft_ok, n)
                pool.tensor_tensor(rot[:], by_cos[:].rearrange("p h d -> p (h d)"),
                                   by_sin[:].rearrange("p h d -> p (h d)"), ALU.add).then_inc(rot_ok, 1)

            rstd_of(0, 0)

            def tile(n, u):
                if not (isinstance(n, int) and n == TILES - 1):
                    rstd_of(n + 1, 1 - u)
                rotate(n, u)
            by_pairs(pool, TILES, tile)

        @block.scalar
        def _(act):
            for n, (_, _, col) in enumerate(weights):
                act.wait_ge(w_tp, n + 1)
                act.activation(w_hi[:, :, col:col + P], tp[:].rearrange("p (k c) -> p k c", k=KT),
                               ACT.Copy).then_inc(w_hi_ok, 1)

            def x_hi(n, u):
                act.wait_ge(tp_ok, n + 1)
                if not before(n, 2):
                    act.wait_ge(mm_ok, BANKS * (n - 1))
                act.activation(xt_hi[:, u].rearrange("p k c -> p (k c)"), tp[:], ACT.Copy).then_inc(xh_ok, 1)

            def v_copy(n, u):
                act.wait_ge(cs_ok, BANKS * (n + 1))
                if not before(n, 2):
                    act.wait_ge(v_out[u], 8 * (n - u))
                act.activation(v_t[:, u, :], qkv[:, HID + KVW:QKVW], ACT.Copy).then_inc(v_ok, 1)

            def f_hi_copy(n):
                act.wait_ge(ft_ok, n + 1)
                if not before(n, 1):
                    act.wait_ge(f_out, 64 * n)
                act.activation(f_hi[:].rearrange("p f c -> p (f c)"), ft[:, 0:FT * P], ACT.Copy).then_inc(fh_ok, 1)

            x_hi(0, 0)

            def tile(n, u):
                if not (isinstance(n, int) and n == TILES - 1):
                    x_hi(n + 1, 1 - u)
                if not before(n, 1):
                    f_hi_copy(n - 1)
                v_copy(n, u)
            by_pairs(act, TILES, tile)
            f_hi_copy(TILES - 1)

        @block.tensor
        def _(pe):
            pe.wait_ge(consts_in, 16)
            for n in range(NW):
                pe.wait_ge(w_in[n % 2], 16 * (n // 2 + 1))
                if n:
                    pe.wait_ge(w_hi_ok, n)
                    pe.wait_ge(w_lo_ok, n)
                for k in range(KT):
                    mm = pe.transpose(tp[:, k * P:(k + 1) * P], w_nat[:, n % 2, k * P:(k + 1) * P], ident[:])
                mm.then_inc(w_tp, 1)

            def turn_x(n, u):
                pe.wait_ge(xn_ok, n + 1)
                if before(n, 1):
                    pe.wait_ge(w_hi_ok, NW)
                    pe.wait_ge(w_lo_ok, NW)
                else:
                    pe.wait_ge(xh_ok, n)
                    pe.wait_ge(xl_ok, n)
                for k in range(KT):
                    mm = pe.transpose(tp[:, k * P:(k + 1) * P], x_t[:, u, k * P:(k + 1) * P], ident[:])
                mm.then_inc(tp_ok, 1)

            def products(n, u, c):
                if c == 0:
                    pe.wait_ge(xh_ok, n + 1)
                    pe.wait_ge(xl_ok, n + 1)
                if not before(n, 1):
                    pe.wait_ge(cs_ok, BANKS * (n - 1) + c + 1)
                    if c == BANKS - 1:
                        pe.wait_ge(v_ok, n)
                cols = slice(c * BANK, (c + 1) * BANK)
                for k in range(KT):
                    mm = three_passes(pe, qkv[:, cols], xt_hi[:, u, k, :], xt_lo[:, u, k, :],
                                      w_hi[:, k, cols], w_lo[:, k, cols], k == 0, k == KT - 1)
                mm.then_inc(mm_ok, 1)

            def turn_f(n):
                pe.wait_ge(rot_ok, n + 1)
                if not before(n, 1):
                    pe.wait_ge(fh_ok, n)
                    pe.wait_ge(fl_ok, n)
                for f in range(FT):
                    mm = pe.transpose(ft[:, f * P:(f + 1) * P], rot[:, f * P:(f + 1) * P], ident[:])
                mm.then_inc(ft_ok, 1)

            turn_x(0, 0)

            def tile(n, u):
                products(n, u, 0)
                if not (isinstance(n, int) and n == TILES - 1):
                    turn_x(n + 1, 1 - u)
                products(n, u, 1)
                if not before(n, 1):
                    turn_f(n - 1)
                products(n, u, 2)
            by_pairs(pe, TILES, tile)
            turn_f(TILES - 1)

        @block.vector
        def _(dve):
            for n, (_, _, col) in enumerate(weights):
                dve.wait_ge(w_hi_ok, n + 1)
                dve.tensor_tensor(w_lo[:, :, col:col + P], tp[:].rearrange("p (k c) -> p k c", k=KT),
                                  w_hi[:, :, col:col + P].bitcast(F32), ALU.subtract).then_inc(w_lo_ok, 1)

            def normalise(n, u):
                dve.wait_ge(x_in[u], 16 * (n - u) + 32)
                for c in range(HID // BANK):
                    dve.bn_stats(bn[:, u, c, :], x_t[:, u, c * BANK:(c + 1) * BANK]).then_inc(bn_ok, 1)
                wait_alone(dve, bn_ok, 2 * n + 2, waited)
                dve.bn_aggr(mean_var[:, u, :], bn[:, u].rearrange("p c s -> p (c s)")).then_inc(agg_ok, 1)
                dve.wait_ge(agg_ok, n + 1)
                dve.wait_ge(rstd_ok, n + 1)
                dve.tensor_scalar(x_t[:, u, :], x_t[:, u, :], mean_var[:, u, 0:1], rstd[:, u:u + 1],
                                  ALU.subtract, ALU.mult).then_inc(xn_ok, 1)

            def x_lo(n, u):
                dve.wait_ge(xh_ok, n + 1)
                dve.tensor_tensor(xt_lo[:, u].rearrange("p k c -> p (k c)"), tp[:],
                                  xt_hi[:, u].rearrange("p k c -> p (k c)").bitcast(F32),
                                  ALU.subtract).then_inc(xl_ok, 1)

            def rotary(n, u, c):
                h0, h1 = heads_in[c]
                dve.wait_ge(mm_ok, BANKS * n + c + 1)
                if c == 0 and not before(n, 1):
                    dve.wait_ge(rot_ok, n)
                q = qkv[:, h0 * HD:h1 * HD].rearrange("p (h d) -> p h d", d=HD)
                table = rope_t[:, u, :]
                wide = lambda a, b: table[:, a:b].unsqueeze(1).broadcast_to([P, h1 - h0, b - a])
                dve.tensor_tensor(by_cos[:, h0:h1, :], q, wide(0, HD), ALU.mult)
                dve.tensor_tensor(by_sin[:, h0:h1, 0:HALF], q[:, :, HALF:HD], wide(HD, HD + HALF), ALU.mult)
                dve.tensor_tensor(by_sin[:, h0:h1, HALF:HD], q[:, :, 0:HALF], wide(HD + HALF, 2 * HD),
                                  ALU.mult).then_inc(cs_ok, 1)

            def f_lo_sub(n):
                dve.wait_ge(fh_ok, n + 1)
                dve.tensor_tensor(f_lo[:].rearrange("p f c -> p (f c)"), ft[:, 0:FT * P],
                                  f_hi[:].rearrange("p f c -> p (f c)").bitcast(F32), ALU.subtract).then_inc(fl_ok, 1)

            normalise(0, 0)
            x_lo(0, 0)

            def tile(n, u):
                if not (isinstance(n, int) and n == TILES - 1):
                    normalise(n + 1, 1 - u)
                rotary(n, u, 0)
                if not (isinstance(n, int) and n == TILES - 1):
                    x_lo(n + 1, 1 - u)
                rotary(n, u, 1)
                if not before(n, 1):
                    f_lo_sub(n - 1)
                rotary(n, u, 2)
            by_pairs(dve, TILES, tile)
            f_lo_sub(TILES - 1)


STEPS = [(c, j) for c in range(CH) for j in range(PER * (c + 1))]


def max_schedule():
    uses = []
    for i in range(KTILES):
        pieces = [("piece", i, h, c) for h in range(GQ) for c in range(i // PER + 1)]
        uses += pieces[:GQ]
        if i:
            uses.append(("turn", i - 1))
        uses += pieces[GQ:]

    def vector_work(use):
        return BANK if use[0] == "turn" or use[3] < use[1] // PER else (use[1] % PER + 1) * P

    def tensor_work(t, slot):
        c, j = STEPS[t]
        wide = BANK - max(0, j - PER * c) * P
        return (2 if slot < 2 else 4) * wide

    slots = [(t, slot) for t in range(FIRST_MAX, len(STEPS) - 2) for slot in range(SLOTS)]
    todo, total = sum(map(vector_work, uses)), sum(tensor_work(*x) for x in slots)
    at, done, passed = {}, 0, 0
    for x in slots:
        passed += tensor_work(*x)
        while uses and (done + vector_work(uses[0]) <= todo * passed / total or x == slots[-1]):
            done += vector_work(uses[0])
            at.setdefault(x, []).append(uses.pop(0))
    at[len(STEPS) - 1, 0] = [("turn", KTILES - 1)]
    return at


FIRST_MAX = 5
SLOTS = 4
USES = max_schedule()
N_USES = sum(len(v) for v in USES.values())
LOADS = 7


def attention(nc, q_s, k_s, v_s, ident_d, mask_d, o_s):
    with ExitStack() as ctx:
        s = Scope(nc, ctx, "p2")
        ident = s.sb("ident", [P, P], F32)
        identr = s.sb("identr", [P, P], F32R)
        identb = s.sb("identb", [P, P], BF16)
        masks_f = s.sb("masks_f", [P, 2, P], F32)
        masks = s.sb("masks", [P, 2, P], BF16)
        ones = s.sb("ones", [P, HD], F32)
        q_st = [s.sb(f"q_st{u}", [P, GQ, SEQ], F32R) for u in range(2)]
        k_st = [s.sb(f"k_st{u}", [P, SEQ], F32R) for u in range(2)]
        v_st = [s.sb(f"v_st{u}", [P, KTILES, HD], F32) for u in range(2)]
        probs = s.sb("probs", [P, 2, GQ, BANK], F32)
        mx = s.sb("mx", [P, 2, GQ, CH], F32)
        neg_max = s.sb("neg_max", [P, 2, GQ], F32)
        stage = s.sb("stage", [P, 2, GQ, KROWS], F32R)
        recip = s.sb("recip", [P, BANK], F32)
        o_n = s.sb("o_n", [P, 2, BANK], F32)
        o_hi = s.sb("o_hi", [P, 2, BANK], F32R)
        o_lo = s.sb("o_lo", [P, 2, BANK], F32R)
        st = s.ps("st", [P, GQ, BANK])
        sm = s.ps("sm", [P, 2, BANK])
        o_ps = s.ps("o", [P, BANK])
        sum_ps = s.ps("sum", [P, BANK])

        consts_in = s.sem("consts_in")
        waited = s.sem("waited")
        set_ok = s.sem("set_ok")
        identr_ok = s.sem("identr_ok")
        loaded = [[s.sem(f"loaded{u}{c}") for c in range(CH)] for u in range(2)]
        sm_ok = s.sem("sm_ok")
        sm_free = s.sem("sm_free")
        m_ok = s.sem("m_ok")
        stage_ok = s.sem("stage_ok")
        mrow_ok = s.sem("mrow_ok")
        st_ok = s.sem("st_ok")
        p_ok = s.sem("p_ok")
        pv_ok = s.sem("pv_ok")
        recip_ok = s.sem("recip_ok")
        norm_ok = s.sem("norm_ok")
        oh_ok = s.sem("oh_ok")
        ol_ok = s.sem("ol_ok")
        o_out = [s.sem("o_out0"), s.sem("o_out1")]

        NS = len(STEPS)

        def by_groups(eng, body):
            with eng.Fori(0, GROUPS // 2 - 1) as i:
                body(2 * i, 0, True)
                body(2 * i + 1, 1, True)
            body(GROUPS - 2, 0, True)
            body(GROUPS - 1, 1, False)

        block = ctx.enter_context(nc.Block())

        @block.sync
        def _(sp):
            sp.dma_start(ident[:], ident_d).then_inc(consts_in, 16)
            sp.dma_start(masks_f[:], mask_d).then_inc(consts_in, 16)

            def load(g, u):
                for c in range(CH):
                    cols = slice(c * BANK, (c + 1) * BANK)
                    batch, kv = g // NKV, g % NKV
                    toks = bass.ds(batch * SEQ + c * BANK, BANK)
                    for row, half in ((0, 0), (HD, 0), (2 * HD, 1)):
                        src = q_s[half, bass.ds(kv * P, P), toks].rearrange("(h d) t -> d h t", d=HD)
                        sp.dma_start(q_st[u][row:row + HD, :, cols].bitcast(F32), src).then_inc(loaded[u][c], 16)
                    for row, half in ((0, 0), (HD, 1), (2 * HD, 0)):
                        sp.dma_start(k_st[u][row:row + HD, cols].bitcast(F32),
                                     k_s[half, bass.ds(kv * HD, HD), toks]).then_inc(loaded[u][c], 16)
                    sp.dma_start(v_st[u][:, c * PER:(c + 1) * PER, :],
                                 v_s[toks, bass.ds(kv * HD, HD)].rearrange("(j p) d -> p j d", p=P)
                                 ).then_inc(loaded[u][c], 16)

            load(0, 0)

            def body(g, u, more):
                if more:
                    wait_alone(sp, pv_ok, NS * g + 2, waited)
                    load(g + 1, 1 - u)
                for c in range(CH):
                    batch, kv = g // NKV, g % NKV
                    toks = bass.ds(batch * SEQ + c * BANK, BANK)
                    for half, o, ready in ((0, o_hi, oh_ok), (1, o_lo, ol_ok)):
                        wait_alone(sp, ready, CH * g + c + 1 + 2 * half, waited)
                        sp.dma_start(o_s[half, bass.ds(kv * P, P), toks],
                                     o[:, c % 2, :].bitcast(F32)).then_inc(o_out[c % 2], 16)
            by_groups(sp, body)
            for k in range(2):
                sp.wait_ge(o_out[k], 32 * (GROUPS * CH // 2 + 1))

        @block.gpsimd
        def _(pool):
            pool.memset(ones[:], 1.0).then_inc(set_ok, 1)
            pool.wait_ge(set_ok, 1)
            pool.memset(stage[:].bitcast(F32), 0.0).then_inc(set_ok, 1)
            for u in range(2):
                pool.wait_ge(set_ok, 2 + u)
                pool.memset(k_st[u][MROW:KROWS, :].bitcast(F32), 1.0).then_inc(set_ok, 1)
            for k in range(2):
                pool.sem_inc(o_out[k], 32)
            pool.sem_inc(ol_ok, 2)

            def body(g, u, more):
                for c in range(CH):
                    n = CH * g + c
                    pool.wait_ge(norm_ok, n + 2)
                    wait_alone(pool, o_out[c % 2], 32 * (CH // 2 * g + c // 2 + 1), waited)
                    pool.tensor_copy(o_hi[:, c % 2, :], o_n[:, c % 2, :]).then_inc(oh_ok, 1)
                    pool.wait_ge(oh_ok, n + 1)
                    pool.tensor_tensor(o_lo[:, c % 2, :], o_n[:, c % 2, :], o_hi[:, c % 2, :].bitcast(F32),
                                       ALU.subtract).then_inc(ol_ok, 1)
            by_groups(pool, body)

        @block.scalar
        def _(act):
            act.sem_inc(p_ok, 2)

            def body(g, u, more):
                for t, (c, j) in enumerate(STEPS):
                    q0 = max(0, j - PER * c) * P
                    for half in range(2):
                        hs = slice(2 * half, 2 * half + 2)
                        act.wait_ge(st_ok, 2 * NS * g + 2 * t + half + 1)
                        if half == 0:
                            act.wait_ge(pv_ok, NS * g + t + 1)
                        act.activation(probs[:, t % 2, hs, q0:BANK], st[:, hs, q0:BANK], ACT.Exp,
                                       scale=SM_SCALE).then_inc(p_ok, 1)
            by_groups(act, body)

        @block.tensor
        def _(pe):
            pe.sem_inc(pv_ok, 2)
            pe.wait_ge(consts_in, 32)
            pe.wait_ge(set_ok, 4)
            pe.wait_ge(identr_ok, 3)

            def use_bank(g, u, n, use):
                at = n % 2
                pe.wait_ge(sm_free, N_USES * g + n + 1)
                if use[0] == "piece":
                    _, i, h, c = use
                    if i % PER == 0 and h == 0 and c == 0:
                        pe.wait_ge(loaded[u][i // PER], 8 * LOADS * (g - u) + 16 * LOADS)
                    diagonal = c == i // PER
                    w = (i % PER + 1) * P if diagonal else BANK
                    mm = pe.matmul(sm[:, at, 0:w], q_st[u][0:MROW, h, i * P:(i + 1) * P],
                                   k_st[u][0:MROW, c * BANK:c * BANK + w], start=True, stop=not diagonal)
                    if diagonal:
                        mm = pe.matmul(sm[:, at, w - P:w], identb[:], masks[:, 0, :], start=False, stop=True)
                else:
                    i = use[1]
                    pe.wait_ge(stage_ok, KTILES * g + i + 1)
                    for h in range(GQ):
                        mm = pe.transpose(sm[0:KROWS, at, h * P:(h + 1) * P].bitcast(F32R),
                                          stage[:, i % 2, h, :], identr[:])
                mm.then_inc(sm_ok, 1)

            def logits(g, u, t, half):
                c, j = STEPS[t]
                q0 = max(0, j - PER * c) * P
                if j == 0 and half == 0:
                    pe.wait_ge(mrow_ok, KTILES * g + PER * (c + 1))
                pe.wait_ge(p_ok, 2 * NS * g + 2 * t + half + 1)
                for h in (2 * half, 2 * half + 1):
                    masked = j >= PER * c
                    mm = pe.matmul(st[:, h, q0:BANK], k_st[u][0:KROWS, j * P:(j + 1) * P],
                                   q_st[u][0:KROWS, h, c * BANK + q0:(c + 1) * BANK],
                                   start=True, stop=not masked)
                    if masked:
                        mm = pe.matmul(st[:, h, q0:q0 + P], identb[:], masks[:, 1, :], start=False, stop=True)
                mm.then_inc(st_ok, 1)

            def weigh(t, out, sta):
                c, j = STEPS[t]
                q0 = max(0, j - PER * c) * P
                for h in range(GQ):
                    mm = pe.matmul(out[h * HD:(h + 1) * HD, q0:BANK], sta, probs[:, t % 2, h, q0:BANK],
                                   start=j == 0, stop=j == PER * (c + 1) - 1)
                return mm

            n = 0
            for t in range(NS):
                for slot in range(SLOTS):
                    for use in USES.get((t, slot), []):
                        use_bank(0, 0, n, use)
                        n += 1

            def body(g, u, more):
                n = 0

                def max_pass(t, slot):
                    nonlocal n
                    for use in USES.get((t, slot), []) if more else []:
                        use_bank(g + 1, 1 - u, n, use)
                        n += 1
                logits(g, u, 0, 0)
                logits(g, u, 0, 1)
                for t, (c, j) in enumerate(STEPS):
                    for half in range(2):
                        max_pass(t, half)
                        if t + 1 < NS:
                            logits(g, u, t + 1, half)
                    max_pass(t, 2)
                    pe.wait_ge(p_ok, 2 * NS * g + 2 * t + 4)
                    if j == 0:
                        pe.wait_ge(norm_ok, CH * g + c + 1)
                    weigh(t, o_ps, v_st[u][:, j, :])
                    max_pass(t, 3)
                    weigh(t, sum_ps, ones[:]).then_inc(pv_ok, 1)
            by_groups(pe, body)

        @block.vector
        def _(dve):
            dve.sem_inc(sm_free, 2)
            dve.sem_inc(norm_ok, 1)
            dve.wait_ge(consts_in, 32)
            dve.tensor_copy(identr[:], ident[:]).then_inc(identr_ok, 1)
            dve.tensor_copy(identb[:], ident[:]).then_inc(identr_ok, 1)
            dve.tensor_copy(masks[:], masks_f[:]).then_inc(identr_ok, 1)
            dve.wait_ge(set_ok, 4)

            def take(g, u, n, use):
                dve.wait_ge(sm_ok, N_USES * g + n + 1)
                if use[0] == "turn":
                    i = use[1]
                    dve.tensor_copy(q_st[u][MROW:KROWS, :, i * P:(i + 1) * P],
                                    sm[MROW:KROWS, n % 2, :].rearrange("r (h q) -> r h q", h=GQ)
                                    ).then_inc(sm_free, 1)
                    dve.wait_ge(sm_free, N_USES * g + n + 3)
                    dve.sem_inc(mrow_ok, 1)
                    return
                _, i, h, c = use
                w = (i % PER + 1) * P if c == i // PER else BANK
                dve.tensor_reduce(mx[:, i % 2, h, c:c + 1], sm[:, n % 2, 0:w], AX.X, ALU.max).then_inc(sm_free, 1)
                if (h, c) == (GQ - 1, i // PER):
                    m = KTILES * g + i
                    dve.wait_ge(sm_free, N_USES * g + n + 3)
                    dve.tensor_reduce(neg_max[:, i % 2, :], mx[:, i % 2, :, 0:c + 1], AX.X, ALU.max,
                                      negate=True).then_inc(m_ok, 1)
                    dve.wait_ge(m_ok, 2 * m + 1)
                    dve.tensor_copy(stage[:, i % 2, :, MROW], neg_max[:, i % 2, :]).then_inc(m_ok, 1)
                    dve.wait_ge(m_ok, 2 * m + 2)
                    dve.tensor_tensor(stage[:, i % 2, :, MROW + 1], neg_max[:, i % 2, :],
                                      stage[:, i % 2, :, MROW].bitcast(F32), ALU.subtract).then_inc(stage_ok, 1)

            def normalise(g, c):
                n = CH * g + c
                dve.wait_ge(pv_ok, NS * g + STEPS.index((c, PER * (c + 1) - 1)) + 3)
                dve.reciprocal(recip[:], sum_ps[:]).then_inc(recip_ok, 1)
                dve.wait_ge(recip_ok, n + 1)
                dve.wait_ge(ol_ok, n + 1)
                dve.tensor_tensor(o_n[:, c % 2, :], o_ps[:], recip[:], ALU.mult).then_inc(norm_ok, 1)

            n = 0
            for t in range(NS):
                for slot in range(SLOTS):
                    for use in USES.get((t, slot), []):
                        take(0, 0, n, use)
                        n += 1

            ends = {STEPS.index((c, PER * (c + 1) - 1)): c for c in range(CH)}

            def body(g, u, more):
                n = 0
                for t in range(NS):
                    for slot in range(SLOTS):
                        if slot == 1 and t - 1 in ends:
                            normalise(g, ends[t - 1])
                        for use in USES.get((t, slot), []) if more else []:
                            take(g + 1, 1 - u, n, use)
                            n += 1
                normalise(g, CH - 1)
            by_groups(dve, body)


def output(nc, x, wo, wb, bias, w_router, lora_a, lora_b, ident_d, iota_d, o_s, out):
    with ExitStack() as ctx:
        s = Scope(nc, ctx, "p3")
        ident = s.sb("ident", [P, P], F32)
        iota = s.sb("iota", [P, EXPERTS], F32)
        bias_t = s.sb("bias", [P, HID], F32)
        wo_hi = s.sb("wo_hi", [P, KT, HID], F32R)
        wo_lo = s.sb("wo_lo", [P, KT, HID], F32R)
        wb_hi = s.sb("wb_hi", [P, KT, HID], F32R)
        wb_lo = s.sb("wb_lo", [P, KT, HID], F32R)
        ar_hi = s.sb("ar_hi", [P, KT, ARW], F32R)
        ar_lo = s.sb("ar_lo", [P, KT, ARW], F32R)
        b_t = s.sb("b_t", [P, HID], F32)
        x_t = s.sb("x", [P, 2, HID], F32)
        res = s.sb("res", [P, 2, HID], F32)
        bn = s.sb("bn", [P, 2, HID // BANK, 6], F32)
        mean_var = s.sb("mean_var", [P, 2, 2], F32)
        var_eps = s.sb("var_eps", [P, 2], F32)
        rstd = s.sb("rstd", [P, 2], F32)
        minus_half = s.sb("minus_half", [P, 1], F32)
        xt_hi = s.sb("xt_hi", [P, 2, KT, P], F32R)
        xt_lo = s.sb("xt_lo", [P, 2, KT, P], F32R)
        o_hi = s.sb("o_hi", [P, 2, KT, P], F32R)
        o_lo = s.sb("o_lo", [P, 2, KT, P], F32R)
        logit = s.sb("logit", [P, EXPERTS], F32)
        top = s.sb("top", [P, 8], F32)
        at = s.sb("at", [P, 8], U32)
        at_f = s.sb("at_f", [P, 2], F32)
        gap = s.sb("gap", [P, 1], F32)
        e_gap = s.sb("e_gap", [P, 1], F32)
        half_sum = s.sb("half_sum", [P, 1], F32)
        w_top = s.sb("w_top", [P, 2], F32)
        gate = s.sb("gate", [P, 2, EXPERTS], F32)
        gates = s.sb("gates", [P, EXPERTS], F32)
        hg = s.sb("hg", [P, ADW], F32)
        hg_t = s.sb("hg_t", [P, P], F32)
        tp = s.ps("tp", [P, KT * P])
        acc = s.ps("acc", [P, 2, HID])
        ar = s.ps("ar", [P, BANK])
        ht = s.ps("ht", [P, BANK])

        consts_in = s.sem("consts_in")
        waited = s.sem("waited")
        w_in = [s.sem("w_in0"), s.sem("w_in1")]
        w_tp = s.sem("w_tp")
        w_hi_ok = s.sem("w_hi_ok")
        w_lo_ok = s.sem("w_lo_ok")
        x_in = [s.sem("x_in0"), s.sem("x_in1")]
        o_in = [s.sem("o_in0"), s.sem("o_in1")]
        bn_ok = s.sem("bn_ok")
        var_ok = s.sem("var_ok")
        eps_ok = s.sem("eps_ok")
        rstd_ok = s.sem("rstd_ok")
        res_ok = s.sem("res_ok")
        xn_ok = s.sem("xn_ok")
        tp_ok = s.sem("tp_ok")
        xh_ok = s.sem("xh_ok")
        xl_ok = s.sem("xl_ok")
        ar_ok = s.sem("ar_ok")
        gap_ok = s.sem("gap_ok")
        e_ok = s.sem("e_ok")
        gate_ok = s.sem("gate_ok")
        hg_ok = s.sem("hg_ok")
        ht_ok = s.sem("ht_ok")
        hgt_ok = s.sem("hgt_ok")
        acc_ok = s.sem("acc_ok")
        out_ok = s.sem("out_ok")
        out_in = [s.sem("out_in0"), s.sem("out_in1")]
        mh_ok = s.sem("mh_ok")
        GATE_STEPS = 8

        weights = [(w[r * P:(r + 1) * P, :], P, hi[:, :, r * P:(r + 1) * P], lo[:, :, r * P:(r + 1) * P])
                   for w, hi, lo in ((wo, wo_hi, wo_lo), (wb, wb_hi, wb_lo)) for r in range(KT)]
        weights.append((lora_a.rearrange("e r d -> (e r) d"), P, ar_hi[:, :, 0:ADW], ar_lo[:, :, 0:ADW]))
        weights.append((w_router, EXPERTS, ar_hi[:, :, ADW:ARW], ar_lo[:, :, ADW:ARW]))
        NW = len(weights)

        block = ctx.enter_context(nc.Block())

        @block.sync
        def _(sp):
            sp.dma_start(ident[:], ident_d).then_inc(consts_in, 16)
            sp.dma_start(iota[:], iota_d).then_inc(consts_in, 16)
            sp.dma_start(bias_t[:], bias.partition_broadcast(P)).then_inc(consts_in, 16)
            for n, (w, rows, _, _) in enumerate(weights):
                if n >= 2:
                    sp.wait_ge(w_tp, n - 1)
                sp.dma_start(x_t[0:rows, n % 2, :], w).then_inc(w_in[n % 2], 16)
            sp.wait_ge(w_tp, NW - 1)
            for k in range(KT):
                sp.dma_start(x_t[:, NW % 2, k * P:(k + 1) * P].rearrange("p (e r) -> p e r", e=EXPERTS),
                             lora_b[:, k * P:(k + 1) * P, :].rearrange("e o r -> o e r")
                             ).then_inc(w_in[NW % 2], 16)

            def load(n, u):
                toks = bass.ds(n * P, P)
                if before(n, 2):
                    sp.wait_ge(w_tp, NW + 1)
                else:
                    wait_alone(sp, tp_ok, n - 1, waited)
                    sp.wait_ge(acc_ok, n - 1)
                sp.dma_start(x_t[:, u, :], x[toks, :]).then_inc(x_in[u], 16)
                for half, o in ((0, o_hi), (1, o_lo)):
                    sp.dma_start(o[:, u].bitcast(F32), o_s[half, :, toks].rearrange("(k p) t -> p k t", p=P)
                                 ).then_inc(o_in[u], 16)

            def store(n, u):
                wait_alone(sp, out_ok, n + 1, waited)
                sp.dma_start(out[bass.ds(n * P, P), :], res[:, u, :]).then_inc(out_in[u], 16)
            load(0, 0)
            load(1, 1)
            by_pairs(sp, TILES - 2, lambda n, u: (load(n + 2, u), store(n, u)))
            store(TILES - 2, 0)
            store(TILES - 1, 1)
            for u in range(2):
                sp.wait_ge(out_in[u], 16 * TILES // 2)

        @block.gpsimd
        def _(pool):
            pool.memset(minus_half[:], -0.5).then_inc(mh_ok, 1)
            pool.wait_ge(mh_ok, 1)
            pool.wait_ge(consts_in, 48)

            def tile(n, u):
                pool.wait_ge(x_in[u], 8 * (n - u) + 16)
                if not before(n, 2):
                    pool.wait_ge(out_in[u], 8 * (n - u))
                pool.tensor_tensor(res[:, u, :], x_t[:, u, :], bias_t[:], ALU.add).then_inc(res_ok, 1)
                wait_alone(pool, var_ok, n + 1, waited)
                pool.tensor_scalar(var_eps[:, u:u + 1], mean_var[:, u, 1:2], EPS, None, ALU.add).then_inc(eps_ok, 1)
                pool.wait_ge(eps_ok, n + 1)
                pool.tensor_tensor(rstd[:, u:u + 1], var_eps[:, u:u + 1], minus_half[:], ALU.pow).then_inc(rstd_ok, 1)
            by_pairs(pool, TILES, tile)

        @block.scalar
        def _(act):
            for n, (_, _, hi, _) in enumerate(weights):
                act.wait_ge(w_tp, n + 1)
                cols = hi.shape[2]
                act.activation(hi, tp[:, 0:KT * cols].rearrange("p (k c) -> p k c", k=KT),
                               ACT.Copy).then_inc(w_hi_ok, 1)
            act.wait_ge(w_tp, NW + 1)
            act.activation(b_t[:], tp[:], ACT.Copy).then_inc(w_hi_ok, 1)

            def x_hi(n, u):
                act.wait_ge(tp_ok, n + 1)
                if not before(n, 2):
                    act.wait_ge(acc_ok, n - 1)
                act.activation(xt_hi[:, u].rearrange("p k c -> p (k c)"), tp[:], ACT.Copy).then_inc(xh_ok, 1)

            x_hi(0, 0)

            def tile(n, u):
                act.wait_ge(gap_ok, n + 1)
                act.activation(e_gap[:], gap[:], ACT.Exp).then_inc(e_ok, 1)
                if not (isinstance(n, int) and n == TILES - 1):
                    x_hi(n + 1, 1 - u)
                act.wait_ge(ht_ok, n + 1)
                if not before(n, 1):
                    act.wait_ge(acc_ok, n)
                act.activation(hg_t[:], ht[:, 0:P], ACT.Copy).then_inc(hgt_ok, 1)
            by_pairs(act, TILES, tile)

        @block.tensor
        def _(pe):
            pe.wait_ge(consts_in, 48)
            for n, (_, rows, hi, _) in enumerate(weights):
                pe.wait_ge(w_in[n % 2], 16 * (n // 2 + 1))
                if n:
                    pe.wait_ge(w_hi_ok, n)
                    pe.wait_ge(w_lo_ok, n)
                for k in range(KT):
                    mm = pe.transpose(tp[:, k * rows:(k + 1) * rows], x_t[0:rows, n % 2, k * P:(k + 1) * P],
                                      ident[0:rows, 0:rows])
                mm.then_inc(w_tp, 1)
            pe.wait_ge(w_in[NW % 2], 16 * (NW // 2 + KT))
            pe.wait_ge(w_hi_ok, NW)
            pe.wait_ge(w_lo_ok, NW)
            for k in range(KT):
                mm = pe.transpose(tp[:, k * P:(k + 1) * P], x_t[:, NW % 2, k * P:(k + 1) * P], ident[:])
            mm.then_inc(w_tp, 1)

            def turn_x(n, u):
                pe.wait_ge(xn_ok, n + 1)
                if before(n, 1):
                    pe.wait_ge(w_hi_ok, NW + 1)
                else:
                    pe.wait_ge(xh_ok, n)
                    pe.wait_ge(xl_ok, n)
                for k in range(KT):
                    mm = pe.transpose(tp[:, k * P:(k + 1) * P], x_t[:, u, k * P:(k + 1) * P], ident[:])
                mm.then_inc(tp_ok, 1)

            def half_products(n, u, c):
                cols = slice(c * BANK, (c + 1) * BANK)
                for k in range(KT):
                    three_passes(pe, acc[:, u, cols], o_hi[:, u, k, :], o_lo[:, u, k, :],
                                 wo_hi[:, k, cols], wo_lo[:, k, cols], k == 0, False)
                for k in range(KT):
                    three_passes(pe, acc[:, u, cols], xt_hi[:, u, k, :], xt_lo[:, u, k, :],
                                 wb_hi[:, k, cols], wb_lo[:, k, cols], False, False)

            turn_x(0, 0)

            def tile(n, u):
                pe.wait_ge(xh_ok, n + 1)
                pe.wait_ge(xl_ok, n + 1)
                if not before(n, 1):
                    pe.wait_ge(hg_ok, n)
                for k in range(KT):
                    mm = three_passes(pe, ar[:, 0:ARW], xt_hi[:, u, k, :], xt_lo[:, u, k, :],
                                      ar_hi[:, k, :], ar_lo[:, k, :], k == 0, k == KT - 1)
                mm.then_inc(ar_ok, 1)
                pe.wait_ge(o_in[u], 16 * (n - u) + 32)
                if not before(n, 2):
                    pe.wait_ge(out_ok, n - 1)
                half_products(n, u, 0)
                if not (isinstance(n, int) and n == TILES - 1):
                    turn_x(n + 1, 1 - u)
                pe.wait_ge(hg_ok, n + 1)
                if not before(n, 1):
                    pe.wait_ge(hgt_ok, n)
                pe.transpose(ht[:, 0:P], hg[:], ident[:]).then_inc(ht_ok, 1)
                half_products(n, u, 1)
                pe.wait_ge(hgt_ok, n + 1)
                for c in range(HID // BANK):
                    cols = slice(c * BANK, (c + 1) * BANK)
                    mm = pe.matmul(acc[:, u, cols], hg_t[:], b_t[:, cols], start=False, stop=True)
                mm.then_inc(acc_ok, 1)
            by_pairs(pe, TILES, tile)

        @block.vector
        def _(dve):
            dve.wait_ge(consts_in, 48)
            for n, (_, _, hi, lo) in enumerate(weights):
                cols = hi.shape[2]
                dve.wait_ge(w_hi_ok, n + 1)
                dve.tensor_tensor(lo, tp[:, 0:KT * cols].rearrange("p (k c) -> p k c", k=KT),
                                  hi.bitcast(F32), ALU.subtract).then_inc(w_lo_ok, 1)

            def normalise(n, u):
                dve.wait_ge(x_in[u], 8 * (n - u) + 16)
                for c in range(HID // BANK):
                    dve.bn_stats(bn[:, u, c, :], x_t[:, u, c * BANK:(c + 1) * BANK]).then_inc(bn_ok, 1)
                wait_alone(dve, bn_ok, 2 * n + 2, waited)
                dve.bn_aggr(mean_var[:, u, :], bn[:, u].rearrange("p c s -> p (c s)")).then_inc(var_ok, 1)
                dve.wait_ge(var_ok, n + 1)
                dve.wait_ge(rstd_ok, n + 1)
                dve.wait_ge(res_ok, n + 1)
                dve.tensor_scalar(x_t[:, u, :], x_t[:, u, :], mean_var[:, u, 0:1], rstd[:, u:u + 1],
                                  ALU.subtract, ALU.mult).then_inc(xn_ok, 1)

            def x_lo(n, u):
                dve.wait_ge(xh_ok, n + 1)
                dve.tensor_tensor(xt_lo[:, u].rearrange("p k c -> p (k c)"), tp[:],
                                  xt_hi[:, u].rearrange("p k c -> p (k c)").bitcast(F32),
                                  ALU.subtract).then_inc(xl_ok, 1)

            def route(n):
                step = 0

                def then(ins):
                    nonlocal step
                    step += 1
                    ins.then_inc(gate_ok, 1)
                    wait_alone(dve, gate_ok, GATE_STEPS * n + step, waited)
                dve.wait_ge(ar_ok, n + 1)
                then(dve.tensor_copy(logit[:], ar[:, ADW:ARW]))
                then(dve.max(out=top[:], in_=logit[:]))
                dve.tensor_tensor(gap[:], top[:, 1:2], top[:, 0:1], ALU.subtract).then_inc(gap_ok, 1)
                then(dve.max_index(out=at[:], in_max=top[:], in_values=logit[:]))
                dve.tensor_copy(at_f[:], at[:, 0:2])
                dve.wait_ge(e_ok, n + 1)
                then(dve.tensor_scalar(half_sum[:], e_gap[:], 1.0, 1.0 / LORA_SCALE, ALU.add, ALU.mult))
                then(dve.reciprocal(w_top[:, 0:1], half_sum[:]))
                then(dve.tensor_tensor(w_top[:, 1:2], w_top[:, 0:1], e_gap[:], ALU.mult))
                for k in range(2):
                    ins = dve.tensor_scalar(gate[:, k, :], iota[:], at_f[:, k:k + 1], w_top[:, k:k + 1],
                                            ALU.is_equal, ALU.mult)
                then(ins)
                then(dve.tensor_tensor(gates[:], gate[:, 0, :], gate[:, 1, :], ALU.add))
                dve.tensor_tensor(hg[:].rearrange("p (e r) -> p e r", e=EXPERTS),
                                  ar[:, 0:ADW].rearrange("p (e r) -> p e r", e=EXPERTS),
                                  gates[:].unsqueeze(2).broadcast_to([P, EXPERTS, RANK]),
                                  ALU.mult).then_inc(hg_ok, 1)
                assert step == GATE_STEPS

            def finish(n, u):
                dve.wait_ge(acc_ok, n + 1)
                dve.tensor_tensor(res[:, u, :], acc[:, u, :], res[:, u, :], ALU.add).then_inc(out_ok, 1)

            normalise(0, 0)
            x_lo(0, 0)

            def tile(n, u):
                if not before(n, 1):
                    finish(n - 1, 1 - u)
                route(n)
                if not (isinstance(n, int) and n == TILES - 1):
                    normalise(n + 1, 1 - u)
                    x_lo(n + 1, 1 - u)
            by_pairs(dve, TILES, tile)
            finish(TILES - 1, 1)


def build(nc, ins, out):
    def scratch(name, shape):
        return nc.dram_tensor(name, shape, F32, kind="Internal").ap()
    q_s = scratch("q_halves", [2, HID, TOKENS])
    k_s = scratch("k_halves", [2, KVW, TOKENS])
    v_s = scratch("v_rows", [TOKENS, KVW])
    o_s = scratch("o_halves", [2, HID, TOKENS])
    x = ins["L0_attn_hidden_states"].rearrange("b s d -> (b s) d")
    project_qkv(nc, x, ins["L0_attn_Wq"], ins["L0_attn_Wk"], ins["L0_attn_Wv"], ins["rope"], ins["ident"],
                q_s, k_s, v_s)
    attention(nc, q_s, k_s, v_s, ins["ident"], ins["masks"], o_s)
    output(nc, x, ins["L0_attn_Wo"], ins["L0_ffn_W_base"], ins["L0_ffn_b_base"], ins["L0_ffn_W_router"],
           ins["L0_ffn_lora_A"], ins["L0_ffn_lora_B"], ins["ident"], ins["iota"], o_s,
           out.rearrange("b s d -> (b s) d"))


def constants():
    import numpy as np

    inv_freq = (1.0 / np.float32(10000.0) ** (np.arange(0, HD, 2, dtype=np.float32) / np.float32(HD))).astype(np.float32)
    angle = np.outer(np.arange(SEQ, dtype=np.float32), inv_freq).astype(np.float32)
    cos, sin = np.cos(angle), np.sin(angle)
    row = np.concatenate([cos, cos, -sin, sin], axis=1).astype(np.float32)
    order = np.arange(P)
    hidden = np.where(order[None, :] <= order[:, None], 0.0, -1e30)
    return {
        "rope": np.ascontiguousarray(np.tile(row, (BATCH, 1))),
        "ident": np.eye(P, dtype=np.float32),
        "masks": np.stack([hidden, hidden.T], axis=1).astype(np.float32),
        "iota": np.tile(np.arange(EXPERTS, dtype=np.float32), (P, 1)),
    }


def kernel(**inputs):
    import numpy as np
    import concourse.bacc as bacc
    from concourse.bass_utils import run_bass_kernel_spmd

    nc = bacc.Bacc("TRN2", target_bir_lowering=False, num_devices=1)
    arrays, ins = {}, {}
    for name, value in {**inputs, **constants()}.items():
        a = np.ascontiguousarray(value)
        arrays[f"in_{name}"] = a
        ins[name] = nc.dram_tensor(f"in_{name}", a.shape, mybir.dt.from_np(a.dtype), kind="ExternalInput").ap()
    out = nc.dram_tensor("out_dram", (BATCH, SEQ, HID), F32, kind="ExternalOutput").ap()
    build(nc, ins, out)
    r = run_bass_kernel_spmd(nc, [arrays], core_ids=[0])
    return r.results[0]["out_dram"]
```

```python
from contextlib import ExitStack

import concourse.bass as bass
from concourse import mybir

F32 = mybir.dt.float32
F32R = mybir.dt.float32r
BF16 = mybir.dt.bfloat16
U32 = mybir.dt.uint32
ALU = mybir.AluOpType
ACT = mybir.ActivationFunctionType
AX = mybir.AxisListType

P = 128
BATCH, SEQ, HID = 2, 2048, 1024
NH, NKV, HD = 32, 8, 32
GQ = NH // NKV
HALF = HD // 2
EXPERTS, RANK = 8, 16
TOKENS = BATCH * SEQ
TILES = TOKENS // P
KT = HID // P
KVW = NKV * HD
QKVW = HID + 2 * KVW
BANK = 512
QKH = NH + NKV
FT = QKH * HD // P
GROUPS = BATCH * NKV
CH = SEQ // BANK
KTILES = SEQ // P
PER = BANK // P
EPS = 1e-5
SM_SCALE = float(HD) ** -0.5
LORA_SCALE = 2.0
MROW = 3 * HD
KROWS = MROW + 2
ADW = EXPERTS * RANK
ARW = ADW + EXPERTS


class Scope:

    def __init__(self, nc, ctx, tag):
        self.nc, self.ctx, self.tag = nc, ctx, tag

    def sb(self, name, shape, dtype):
        return self.ctx.enter_context(self.nc.sbuf_tensor(f"{self.tag}_{name}", shape, dtype))

    def ps(self, name, shape, dtype=F32):
        return self.ctx.enter_context(self.nc.psum_tensor(f"{self.tag}_{name}", shape, dtype))

    def sem(self, name):
        return self.ctx.enter_context(self.nc.semaphore(f"{self.tag}_{name}"))


def by_pairs(eng, count, tile):
    tile(0, 0)
    tile(1, 1)
    with eng.Fori(1, count // 2 - 1) as i:
        tile(2 * i, 0)
        tile(2 * i + 1, 1)
    tile(count - 2, 0)
    tile(count - 1, 1)


def before(n, k):
    return isinstance(n, int) and n < k


def wait_alone(eng, sem, value, waited):
    eng.wait_ge(sem, value)
    eng.sem_inc(waited, 1)


def three_passes(pe, out, sta_hi, sta_lo, mov_hi, mov_lo, first, last):
    pe.matmul(out, sta_hi, mov_hi, start=first, stop=False)
    pe.matmul(out, sta_hi, mov_lo, start=False, stop=False)
    return pe.matmul(out, sta_lo, mov_hi, start=False, stop=last)


def project_qkv(nc, x, wq, wk, wv, rope, ident_d, q_s, k_s, v_s):
    with ExitStack() as ctx:
        s = Scope(nc, ctx, "p1")
        NAT = 4
        ident = s.sb("ident", [P, P], F32)
        w_nat = s.sb("w_nat", [P, NAT, HID], F32)
        w_hi = s.sb("w_hi", [P, KT, QKVW], F32R)
        w_lo = s.sb("w_lo", [P, KT, QKVW], F32R)
        x_t = s.sb("x", [P, 2, HID], F32)
        rope_t = s.sb("rope", [P, TILES, 2 * HD], F32)
        bn = s.sb("bn", [P, 2, HID // BANK, 6], F32)
        mean_var = s.sb("mean_var", [P, 2, 2], F32)
        var_eps = s.sb("var_eps", [P, 2], F32)
        rstd = s.sb("rstd", [P, 2], F32)
        minus_half = s.sb("minus_half", [P, 1], F32)
        xt_hi = s.sb("xt_hi", [P, 2, KT, P], F32R)
        xt_lo = s.sb("xt_lo", [P, 2, KT, P], F32R)
        by_cos = s.sb("by_cos", [P, QKH, HD], F32)
        by_sin = s.sb("by_sin", [P, QKH, HD], F32)
        rot = s.sb("rot", [P, QKH * HD], F32)
        v_t = s.sb("v", [P, 2, KVW], F32)
        f_hi = s.sb("f_hi", [P, FT, P], F32R)
        f_lo = s.sb("f_lo", [P, FT, P], F32R)
        tp = s.ps("tp", [P, KT * P])
        qkv = s.ps("qkv", [P, QKVW])
        ft = s.ps("ft", [P, 3 * BANK])

        consts_in = s.sem("consts_in")
        waited = s.sem("waited")
        w_in = [s.sem(f"w_in{k}") for k in range(NAT)]
        w_tp = s.sem("w_tp")
        w_hi_ok = s.sem("w_hi_ok")
        w_lo_ok = s.sem("w_lo_ok")
        rope_in = s.sem("rope_in")
        x_in = [s.sem("x_in0"), s.sem("x_in1")]
        bn_ok = s.sem("bn_ok")
        agg_ok = s.sem("agg_ok")
        eps_ok = s.sem("eps_ok")
        rstd_ok = s.sem("rstd_ok")
        xn_ok = s.sem("xn_ok")
        tp_ok = s.sem("tp_ok")
        xh_ok = s.sem("xh_ok")
        xl_ok = s.sem("xl_ok")
        mm_ok = s.sem("mm_ok")
        cs_ok = s.sem("cs_ok")
        v_ok = s.sem("v_ok")
        rot_ok = s.sem("rot_ok")
        ft_ok = s.sem("ft_ok")
        fh_ok = s.sem("fh_ok")
        fl_ok = s.sem("fl_ok")
        f_out = s.sem("f_out")
        v_out = [s.sem("v_out0"), s.sem("v_out1")]
        mh_ok = s.sem("mh_ok")

        weights = [(wq, r, r * P) for r in range(HID // P)]
        weights += [(wk, r, HID + r * P) for r in range(KVW // P)]
        weights += [(wv, r, HID + KVW + r * P) for r in range(KVW // P)]
        NW = len(weights)
        BANKS = QKVW // BANK
        heads_in = [(c * BANK // HD, min((c + 1) * BANK // HD, QKH)) for c in range(BANKS)]

        w_ps = [tp[:], qkv[:, 0:KT * P]]

        block = ctx.enter_context(nc.Block())

        @block.sync
        def _(sp):
            sp.dma_start(ident[:], ident_d).then_inc(consts_in, 16)

            def load(n, u):
                if not before(n, 2):
                    wait_alone(sp, tp_ok, n - 1, waited)
                sp.dma_start(x_t[:, u, :], x[bass.ds(n * P, P), :]).then_inc(x_in[u], 16)

            for n, (w, r, _) in enumerate(weights):
                if n >= NAT:
                    sp.wait_ge(w_tp, n - NAT + 1)
                sp.dma_start(w_nat[:, n % NAT, :], w[r * P:(r + 1) * P, :]).then_inc(w_in[n % NAT], 16)
                if n == NAT:
                    sp.dma_start(rope_t[:], rope).then_inc(rope_in, 16)
                    load(0, 0)
                    load(1, 1)

            def store(n, u):
                toks = bass.ds(n * P, P)
                wait_alone(sp, v_ok, n + 1, waited)
                sp.dma_start(v_s[toks, :], v_t[:, u, :]).then_inc(v_out[u], 16)
                for half, f, ready in ((0, f_hi, fh_ok), (1, f_lo, fl_ok)):
                    wait_alone(sp, ready, n + 1, waited)
                    sp.dma_start(q_s[half, :, toks].rearrange("(f p) t -> p f t", p=P),
                                 f[:, 0:HID // P, :].bitcast(F32)).then_inc(f_out, 16)
                    sp.dma_start(k_s[half, :, toks].rearrange("(f p) t -> p f t", p=P),
                                 f[:, HID // P:FT, :].bitcast(F32)).then_inc(f_out, 16)

            load(2, 0)
            by_pairs(sp, TILES - 4, lambda n, u: (load(n + 3, 1 - u), store(n, u)))
            load(TILES - 1, 1)
            for n in range(TILES - 4, TILES):
                store(n, n % 2)
            sp.wait_ge(f_out, 64 * TILES)
            for u in range(2):
                sp.wait_ge(v_out[u], 16 * TILES // 2)

        @block.gpsimd
        def _(pool):
            pool.memset(minus_half[:], -0.5).then_inc(mh_ok, 1)
            pool.wait_ge(mh_ok, 1)

            def rstd_of(n, u):
                wait_alone(pool, agg_ok, n + 1, waited)
                pool.tensor_scalar(var_eps[:, u:u + 1], mean_var[:, u, 1:2], EPS, None, ALU.add).then_inc(eps_ok, 1)
                pool.wait_ge(eps_ok, n + 1)
                pool.tensor_tensor(rstd[:, u:u + 1], var_eps[:, u:u + 1], minus_half[:], ALU.pow).then_inc(rstd_ok, 1)

            def rotate(n, u):
                pool.wait_ge(cs_ok, BANKS * (n + 1))
                if not before(n, 1):
                    pool.wait_ge(ft_ok, n)
                pool.tensor_tensor(rot[:], by_cos[:].rearrange("p h d -> p (h d)"),
                                   by_sin[:].rearrange("p h d -> p (h d)"), ALU.add).then_inc(rot_ok, 1)

            rstd_of(0, 0)

            def tile(n, u):
                if not (isinstance(n, int) and n == TILES - 1):
                    rstd_of(n + 1, 1 - u)
                rotate(n, u)
            by_pairs(pool, TILES, tile)

        @block.scalar
        def _(act):
            for n, (_, _, col) in enumerate(weights):
                act.wait_ge(w_tp, n + 1)
                act.activation(w_hi[:, :, col:col + P], w_ps[n % 2].rearrange("p (k c) -> p k c", k=KT),
                               ACT.Copy).then_inc(w_hi_ok, 1)

            def x_hi(n, u):
                act.wait_ge(tp_ok, n + 1)
                if not before(n, 2):
                    act.wait_ge(mm_ok, BANKS * (n - 1))
                act.activation(xt_hi[:, u].rearrange("p k c -> p (k c)"), tp[:], ACT.Copy).then_inc(xh_ok, 1)

            def v_copy(n, u):
                act.wait_ge(cs_ok, BANKS * (n + 1))
                if not before(n, 2):
                    act.wait_ge(v_out[u], 8 * (n - u))
                act.activation(v_t[:, u, :], qkv[:, HID + KVW:QKVW], ACT.Copy).then_inc(v_ok, 1)

            def f_hi_copy(n):
                act.wait_ge(ft_ok, n + 1)
                if not before(n, 1):
                    act.wait_ge(f_out, 64 * n)
                act.activation(f_hi[:].rearrange("p f c -> p (f c)"), ft[:, 0:FT * P], ACT.Copy).then_inc(fh_ok, 1)

            x_hi(0, 0)

            def tile(n, u):
                if not (isinstance(n, int) and n == TILES - 1):
                    x_hi(n + 1, 1 - u)
                if not before(n, 1):
                    f_hi_copy(n - 1)
                v_copy(n, u)
            by_pairs(act, TILES, tile)
            f_hi_copy(TILES - 1)

        @block.tensor
        def _(pe):
            pe.wait_ge(consts_in, 16)
            for n in range(NW):
                pe.wait_ge(w_in[n % NAT], 16 * (n // NAT + 1))
                if n >= 2:
                    pe.wait_ge(w_hi_ok, n - 1)
                    pe.wait_ge(w_lo_ok, n - 1)
                for k in range(KT):
                    mm = pe.transpose(w_ps[n % 2][:, k * P:(k + 1) * P], w_nat[:, n % NAT, k * P:(k + 1) * P], ident[:])
                mm.then_inc(w_tp, 1)

            def turn_x(n, u):
                pe.wait_ge(xn_ok, n + 1)
                if before(n, 1):
                    pe.wait_ge(w_hi_ok, NW)
                    pe.wait_ge(w_lo_ok, NW)
                else:
                    pe.wait_ge(xh_ok, n)
                    pe.wait_ge(xl_ok, n)
                for k in range(KT):
                    mm = pe.transpose(tp[:, k * P:(k + 1) * P], x_t[:, u, k * P:(k + 1) * P], ident[:])
                mm.then_inc(tp_ok, 1)

            def products(n, u, c):
                if c == 0:
                    pe.wait_ge(xh_ok, n + 1)
                    pe.wait_ge(xl_ok, n + 1)
                if not before(n, 1):
                    pe.wait_ge(cs_ok, BANKS * (n - 1) + c + 1)
                    if c == BANKS - 1:
                        pe.wait_ge(v_ok, n)
                cols = slice(c * BANK, (c + 1) * BANK)
                for k in range(KT):
                    mm = three_passes(pe, qkv[:, cols], xt_hi[:, u, k, :], xt_lo[:, u, k, :],
                                      w_hi[:, k, cols], w_lo[:, k, cols], k == 0, k == KT - 1)
                mm.then_inc(mm_ok, 1)

            def turn_f(n):
                pe.wait_ge(rot_ok, n + 1)
                if not before(n, 1):
                    pe.wait_ge(fh_ok, n)
                    pe.wait_ge(fl_ok, n)
                for f in range(FT):
                    mm = pe.transpose(ft[:, f * P:(f + 1) * P], rot[:, f * P:(f + 1) * P], ident[:])
                mm.then_inc(ft_ok, 1)

            turn_x(0, 0)

            def tile(n, u):
                products(n, u, 0)
                if not (isinstance(n, int) and n == TILES - 1):
                    turn_x(n + 1, 1 - u)
                products(n, u, 1)
                if not before(n, 1):
                    turn_f(n - 1)
                products(n, u, 2)
            by_pairs(pe, TILES, tile)
            turn_f(TILES - 1)

        @block.vector
        def _(dve):
            for n, (_, _, col) in enumerate(weights):
                dve.wait_ge(w_hi_ok, n + 1)
                dve.tensor_tensor(w_lo[:, :, col:col + P], w_ps[n % 2].rearrange("p (k c) -> p k c", k=KT),
                                  w_hi[:, :, col:col + P].bitcast(F32), ALU.subtract).then_inc(w_lo_ok, 1)

            def normalise(n, u):
                dve.wait_ge(x_in[u], 8 * (n - u) + 16)
                for c in range(HID // BANK):
                    dve.bn_stats(bn[:, u, c, :], x_t[:, u, c * BANK:(c + 1) * BANK]).then_inc(bn_ok, 1)
                wait_alone(dve, bn_ok, 2 * n + 2, waited)
                dve.bn_aggr(mean_var[:, u, :], bn[:, u].rearrange("p c s -> p (c s)")).then_inc(agg_ok, 1)
                dve.wait_ge(agg_ok, n + 1)
                dve.wait_ge(rstd_ok, n + 1)
                dve.tensor_scalar(x_t[:, u, :], x_t[:, u, :], mean_var[:, u, 0:1], rstd[:, u:u + 1],
                                  ALU.subtract, ALU.mult).then_inc(xn_ok, 1)

            def x_lo(n, u):
                dve.wait_ge(xh_ok, n + 1)
                dve.tensor_tensor(xt_lo[:, u].rearrange("p k c -> p (k c)"), tp[:],
                                  xt_hi[:, u].rearrange("p k c -> p (k c)").bitcast(F32),
                                  ALU.subtract).then_inc(xl_ok, 1)

            def rotary(n, u, c):
                h0, h1 = heads_in[c]
                dve.wait_ge(mm_ok, BANKS * n + c + 1)
                if c == 0 and not before(n, 1):
                    dve.wait_ge(rot_ok, n)
                q = qkv[:, h0 * HD:h1 * HD].rearrange("p (h d) -> p h d", d=HD)
                table = rope_t[:, bass.ds(n, 1), :]
                wide = lambda a, b: table[:, :, a:b].broadcast_to([P, h1 - h0, b - a])
                dve.tensor_tensor(by_cos[:, h0:h1, :], q, wide(0, HD), ALU.mult)
                dve.tensor_tensor(by_sin[:, h0:h1, 0:HALF], q[:, :, HALF:HD], wide(HD, HD + HALF), ALU.mult)
                dve.tensor_tensor(by_sin[:, h0:h1, HALF:HD], q[:, :, 0:HALF], wide(HD + HALF, 2 * HD),
                                  ALU.mult).then_inc(cs_ok, 1)

            def f_lo_sub(n):
                dve.wait_ge(fh_ok, n + 1)
                dve.tensor_tensor(f_lo[:].rearrange("p f c -> p (f c)"), ft[:, 0:FT * P],
                                  f_hi[:].rearrange("p f c -> p (f c)").bitcast(F32), ALU.subtract).then_inc(fl_ok, 1)

            normalise(0, 0)
            x_lo(0, 0)
            dve.wait_ge(rope_in, 16)

            def tile(n, u):
                if not (isinstance(n, int) and n == TILES - 1):
                    normalise(n + 1, 1 - u)
                rotary(n, u, 0)
                if not (isinstance(n, int) and n == TILES - 1):
                    x_lo(n + 1, 1 - u)
                rotary(n, u, 1)
                if not before(n, 1):
                    f_lo_sub(n - 1)
                rotary(n, u, 2)
            by_pairs(dve, TILES, tile)
            f_lo_sub(TILES - 1)


STEPS = [(c, j) for c in range(CH) for j in range(PER * (c + 1))]
NS = len(STEPS)
LAST = [STEPS.index((c, PER * (c + 1) - 1)) for c in range(CH)]
SLOTS = 6
RING = 3
HEADS = GQ * NS
CHAIN = 6
AHEAD = 11
NP = 8


COL, VEC_COL, ACT_COL, VEC_FIXED, ACT_FIXED, HOP, NORM = 1 / 2.4, 1.04, 0.83, 80, 60, 60, 600
EARLY, FILLER, LATE = 700, 2000, 3000


def max_order():
    uses, due = [], []
    for i in range(KTILES):
        for h in range(GQ):
            for c in range(i // PER + 1):
                uses.append(("piece", i, h, c))
                if due and due[0][0] == len(uses):
                    uses.append(("turn", due.pop(0)[1]))
        due.append((len(uses) + CHAIN, i))
    assert len(due) == 1
    return uses + [("turn", KTILES - 1)]


ORDER = max_order()
N_USES = len(ORDER)
N_PIECES = sum(use[0] == "piece" for use in ORDER)
HEAD = ORDER.index(("turn", AHEAD - 1)) + 1


def freed(n):
    if n < RING:
        return ORDER[max(range(n, N_USES, RING))][0], 0
    kind = ORDER[n - RING][0]
    return kind, sum(use[0] == kind for use in ORDER[:n - RING + 1])


def head_freed(k):
    return k - RING + 1 if k >= RING else max(range(k, HEADS, RING)) + 1 - HEADS


def piece_width(use):
    _, i, _, c = use
    return (i % PER + 1) * P if c == i // PER else BANK


def max_schedule():
    uses = [(0, n, ORDER[n]) for n in range(HEAD, N_USES)] + [(1, n, ORDER[n]) for n in range(HEAD)]
    slots = [(t, slot) for t in range(NS) for slot in range(SLOTS)]
    width = [BANK - max(0, j - PER * c) * P for c, j in STEPS]

    def vector_work(use):
        return piece_width(use) * VEC_COL + VEC_FIXED if use[0] == "piece" else 0

    def tensor_work(t, slot):
        if slot in (2, 4):
            return GQ * COL * (width[t] if slot == 4 else sum(width[x] for x in SUMMED.get(t, [])))
        return width[(t + 1) % NS] * COL

    todo, total = sum(vector_work(use) for _, _, use in uses), sum(tensor_work(*x) for x in slots)
    tensor = scalar = vector = done = passed = 0
    free = {HEAD - k: 0 for k in range(1, RING + 1)}
    exp = [0] * (HEADS + GQ)
    staged, schedule, k = {}, {}, HEAD
    for x in slots:
        t, slot = x
        head = GQ * (t + 1) + {0: 0, 1: 1, 3: 2, 5: 3}.get(slot, 0)
        needs = {2: 0, 4: exp[GQ * t + 3]}.get(slot, exp[head - RING])
        if t - 3 in LAST and slot < 4:
            vector = max(vector, tensor) + NORM
        while uses:
            use = uses[0][2]
            work = vector_work(use)
            late = todo * passed / total - done - work
            ready = max(free[k - RING], staged.get(use[1], 0) if use[0] == "turn" else 0)
            waits = needs > tensor + VEC_FIXED
            if x != slots[-1] and (late < -(FILLER if waits else EARLY) or
                                   (ready > (needs if waits else tensor) and late < LATE)):
                break
            tensor = max(tensor, ready)
            if use[0] == "piece":
                tensor += piece_width(use) * COL
                vector = max(vector, tensor + HOP) + work
                free[k] = vector + HOP
                if use[2] == GQ - 1 and use[3] == use[1] // PER:
                    staged[use[1]] = vector + 3 * 2 * VEC_FIXED
                    vector += 3 * VEC_FIXED
            else:
                tensor += BANK * COL
                scalar = max(scalar, tensor + HOP) + BANK * ACT_COL + ACT_FIXED
                free[k] = scalar + HOP
            done += work
            k += 1
            schedule.setdefault(x, []).append(uses.pop(0))
        tensor = max(tensor, needs) + tensor_work(t, slot)
        passed += tensor_work(t, slot)
        if slot not in (2, 4):
            scalar = max(scalar, tensor + HOP) + width[(t + 1) % NS] * ACT_COL + ACT_FIXED
            exp[head] = scalar + HOP
    assert not uses
    for (t, _), here in schedule.items():
        for nxt, _, use in here:
            if use[0] == "turn" and nxt == 0:
                assert t + 1 < STEPS.index((use[1] // PER, 0)), "turned in time for its chunk"
    return schedule


def sum_schedule():
    added, summed = {}, {}
    for c in range(CH):
        for j in range(0, PER * (c + 1), PER):
            t = STEPS.index((c, j))
            if c == CH - 1 and j == PER * c:
                for k in range(PER):
                    summed.setdefault(t + k + 1, []).append(t + k)
                continue
            whole = j < PER * c
            for k in range(1, PER):
                added[t + k] = t
            summed.setdefault(t + 5 + whole, []).append(t)
    return added, summed


ADDED, SUMMED = sum_schedule()
USES = max_schedule()
SUM_ORDER = [(n, x) for n in sorted(SUMMED) for x in SUMMED[n]]
ADDS = sorted(ADDED)
N_V = NS + 1
LOADS = 7


def attention(nc, q_s, k_s, v_s, ident_d, mask_d, o_s):
    with ExitStack() as ctx:
        s = Scope(nc, ctx, "p2")
        ident = s.sb("ident", [P, P], F32)
        identr = s.sb("identr", [P, P], F32R)
        identb = s.sb("identb", [P, P], BF16)
        masks_f = s.sb("masks_f", [P, 2, P], F32)
        masks = s.sb("masks", [P, 2, P], BF16)
        ones = s.sb("ones", [P, HD], F32)
        q_st = [s.sb(f"q_st{u}", [P, GQ, SEQ], F32R) for u in range(2)]
        k_st = [s.sb(f"k_st{u}", [P, SEQ], F32R) for u in range(2)]
        v_st = [s.sb(f"v_st{u}", [P, KTILES, HD], F32) for u in range(2)]
        probs = s.sb("probs", [P, NP, GQ, BANK], F32)
        mx = s.sb("mx", [P, 2, GQ, CH], F32)
        neg_max = s.sb("neg_max", [P, 2, GQ], F32)
        stage = s.sb("stage", [P, 2, GQ, KROWS], F32R)
        o_raw = s.sb("o_raw", [P, BANK], F32)
        sum_t = s.sb("sum_t", [P, BANK], F32)
        recip_t = s.sb("recip_t", [P, BANK // HD], F32)
        recip = s.sb("recip", [P, BANK], F32)
        o_n = s.sb("o_n", [P, 2, BANK], F32)
        o_hi = s.sb("o_hi", [P, 2, BANK], F32R)
        o_lo = s.sb("o_lo", [P, 2, BANK], F32R)
        st = s.ps("st", [P, RING, BANK])
        sm = s.ps("sm", [P, RING, BANK])
        o_ps = s.ps("o", [P, BANK])
        sum_ps = s.ps("sum", [P, BANK])

        consts_in = s.sem("consts_in")
        waited = s.sem("waited")
        set_ok = s.sem("set_ok")
        cast_ok = s.sem("cast_ok")
        loaded = [[s.sem(f"loaded{u}{c}") for c in range(CH)] for u in range(2)]
        sm_ok = s.sem("sm_ok")
        piece_used = s.sem("piece_used")
        turn_used = s.sem("turn_used")
        m_ok = s.sem("m_ok")
        stage_ok = s.sem("stage_ok")
        st_ok = s.sem("st_ok")
        p_ok = s.sem("p_ok")
        v_ok = s.sem("v_ok")
        add_ok = s.sem("add_ok")
        o_left = s.sem("o_left")
        sum_left = s.sem("sum_left")
        recip_ok = s.sem("recip_ok")
        norm_ok = s.sem("norm_ok")
        oh_ok = s.sem("oh_ok")
        ol_ok = s.sem("ol_ok")
        o_out = [s.sem("o_out0"), s.sem("o_out1")]

        def by_groups(eng, body):
            with eng.Fori(0, GROUPS // 2 - 1) as i:
                body(2 * i, 0, True)
                body(2 * i + 1, 1, True)
            body(GROUPS - 2, 0, True)
            body(GROUPS - 1, 1, False)

        def probs_of(g, t):
            return HEADS * g + GQ * (t + 1) + RING

        def steps_done(g, t):
            return N_V * g + t + 1 + NP

        block = ctx.enter_context(nc.Block())

        @block.sync
        def _(sp):
            sp.dma_start(ident[:], ident_d).then_inc(consts_in, 16)
            sp.dma_start(masks_f[:], mask_d).then_inc(consts_in, 16)

            def load(g, u):
                for c in range(CH):
                    cols = slice(c * BANK, (c + 1) * BANK)
                    batch, kv = g // NKV, g % NKV
                    toks = bass.ds(batch * SEQ + c * BANK, BANK)
                    for row, half in ((0, 0), (HD, 0), (2 * HD, 1)):
                        src = q_s[half, bass.ds(kv * P, P), toks].rearrange("(h d) t -> d h t", d=HD)
                        sp.dma_start(q_st[u][row:row + HD, :, cols].bitcast(F32), src).then_inc(loaded[u][c], 16)
                    for row, half in ((0, 0), (HD, 1), (2 * HD, 0)):
                        sp.dma_start(k_st[u][row:row + HD, cols].bitcast(F32),
                                     k_s[half, bass.ds(kv * HD, HD), toks]).then_inc(loaded[u][c], 16)
                    sp.dma_start(v_st[u][:, c * PER:(c + 1) * PER, :],
                                 v_s[toks, bass.ds(kv * HD, HD)].rearrange("(j p) d -> p j d", p=P)
                                 ).then_inc(loaded[u][c], 16)

            load(0, 0)

            def body(g, u, more):
                if more:
                    wait_alone(sp, v_ok, N_V * g + NP, waited)
                    load(g + 1, 1 - u)
                for c in range(CH):
                    batch, kv = g // NKV, g % NKV
                    toks = bass.ds(batch * SEQ + c * BANK, BANK)
                    for half, o, ready in ((0, o_hi, oh_ok), (1, o_lo, ol_ok)):
                        wait_alone(sp, ready, CH * g + c + 1 + 2 * half, waited)
                        sp.dma_start(o_s[half, bass.ds(kv * P, P), toks],
                                     o[:, c % 2, :].bitcast(F32)).then_inc(o_out[c % 2], 16)
            by_groups(sp, body)
            for k in range(2):
                sp.wait_ge(o_out[k], 32 * (GROUPS * CH // 2 + 1))

        @block.gpsimd
        def _(pool):
            pool.memset(ones[:], 1.0).then_inc(set_ok, 1)
            pool.wait_ge(set_ok, 1)
            pool.memset(stage[:].bitcast(F32), 0.0).then_inc(set_ok, 1)
            for u in range(2):
                pool.wait_ge(set_ok, 2 + u)
                pool.memset(k_st[u][MROW:KROWS, :].bitcast(F32), 1.0).then_inc(set_ok, 1)
            for k in range(2):
                pool.sem_inc(o_out[k], 32)
            pool.sem_inc(ol_ok, 2)

            def halves(g, c):
                n = CH * g + c
                pool.wait_ge(norm_ok, n + 1)
                wait_alone(pool, o_out[c % 2], 32 * (CH // 2 * g + c // 2 + 1), waited)
                pool.tensor_copy(o_hi[:, c % 2, :], o_n[:, c % 2, :]).then_inc(oh_ok, 1)
                pool.wait_ge(oh_ok, n + 1)
                pool.tensor_tensor(o_lo[:, c % 2, :], o_n[:, c % 2, :], o_hi[:, c % 2, :].bitcast(F32),
                                   ALU.subtract).then_inc(ol_ok, 1)

            def body(g, u, more):
                for t in range(NS):
                    if t in ADDED:
                        c, j = STEPS[t]
                        q0 = max(0, j - PER * c) * P
                        total = probs[:, ADDED[t] % NP, :, q0:BANK]
                        k = len(ADDS) * g + ADDS.index(t)
                        pool.wait_ge(p_ok, probs_of(g, t))
                        if t == ADDED[t] + 1:
                            pool.wait_ge(v_ok, steps_done(g, ADDED[t]))
                        else:
                            pool.wait_ge(add_ok, k)
                        pool.tensor_tensor(total, total, probs[:, t % NP, :, q0:BANK], ALU.add).then_inc(add_ok, 1)
                    if t - 6 in LAST:
                        halves(g, LAST.index(t - 6))
                halves(g, CH - 1)
            by_groups(pool, body)

        @block.scalar
        def _(act):
            act.sem_inc(p_ok, RING)
            act.sem_inc(turn_used, 1)

            def turned(g, u, n, use):
                i = use[1]
                act.wait_ge(sm_ok, N_USES * g + n + 1)
                act.activation(q_st[u][MROW:KROWS, :, i * P:(i + 1) * P],
                               sm[MROW:KROWS, n % RING, :].rearrange("r (h q) -> r h q", h=GQ),
                               ACT.Copy).then_inc(turn_used, 1)

            for n, use in enumerate(ORDER[:HEAD]):
                if use[0] == "turn":
                    turned(0, 0, n, use)

            def body(g, u, more):
                def turns(t, slots):
                    for slot in slots:
                        for nxt, n, use in USES.get((t, slot), []):
                            if use[0] == "turn" and (more or not nxt):
                                turned(g + nxt, (u + nxt) % 2, n, use)
                for t, (c, j) in enumerate(STEPS):
                    q0 = max(0, j - PER * c) * P
                    for h in range(GQ):
                        if t:
                            turns(t - 1, [[0], [1], [2, 3], [4, 5]][h])
                        if h == 3 and t - 1 in LAST:
                            act.wait_ge(v_ok, steps_done(g, t - 1))
                            act.wait_ge(norm_ok, CH * g + LAST.index(t - 1))
                            act.activation(o_raw[:], o_ps[:], ACT.Copy).then_inc(o_left, 1)
                        k = GQ * t + h
                        act.wait_ge(st_ok, HEADS * g + k + 1)
                        if h == 0:
                            act.wait_ge(v_ok, steps_done(g, t - 2))
                        act.activation(probs[:, t % NP, h, q0:BANK], st[:, k % RING, q0:BANK], ACT.Exp,
                                       scale=SM_SCALE).then_inc(p_ok, 1)
                turns(NS - 1, range(SLOTS))
            by_groups(act, body)

        @block.tensor
        def _(pe):
            pe.sem_inc(v_ok, NP)
            pe.wait_ge(consts_in, 32)
            pe.wait_ge(set_ok, 4)
            pe.wait_ge(cast_ok, 3)

            def use_bank(g, u, n, use):
                at = n % RING
                kind, count = freed(n)
                if kind == "piece":
                    pe.wait_ge(piece_used, 2 * N_PIECES * g + 2 * count + 1)
                else:
                    pe.wait_ge(turn_used, KTILES * g + count + 1)
                if use[0] == "piece":
                    _, i, h, c = use
                    if i % PER == 0 and h == 0 and c == 0:
                        pe.wait_ge(loaded[u][i // PER], 8 * LOADS * (g - u) + 16 * LOADS)
                    diagonal = c == i // PER
                    w = piece_width(use)
                    mm = pe.matmul(sm[:, at, 0:w], q_st[u][0:MROW, h, i * P:(i + 1) * P],
                                   k_st[u][0:MROW, c * BANK:c * BANK + w], start=True, stop=not diagonal)
                    if diagonal:
                        mm = pe.matmul(sm[:, at, w - P:w], identb[:], masks[:, 0, :], start=False, stop=True)
                else:
                    i = use[1]
                    pe.wait_ge(stage_ok, KTILES * g + i + 1)
                    for h in range(GQ):
                        mm = pe.transpose(sm[0:KROWS, at, h * P:(h + 1) * P].bitcast(F32R),
                                          stage[:, i % 2, h, :], identr[:])
                mm.then_inc(sm_ok, 1)

            def logits(g, u, t, h):
                c, j = STEPS[t]
                k, q0 = GQ * t + h, max(0, j - PER * c) * P
                if j == 0 and h == 0:
                    pe.wait_ge(turn_used, KTILES * g + PER * (c + 1) + 1)
                pe.wait_ge(p_ok, HEADS * g + head_freed(k) + RING)
                masked = j >= PER * c
                mm = pe.matmul(st[:, k % RING, q0:BANK], k_st[u][0:KROWS, j * P:(j + 1) * P],
                               q_st[u][0:KROWS, h, c * BANK + q0:(c + 1) * BANK], start=True, stop=not masked)
                if masked:
                    mm = pe.matmul(st[:, k % RING, q0:q0 + P], identb[:], masks[:, 1, :], start=False, stop=True)
                mm.then_inc(st_ok, 1)

            def weigh(t, out, sta, first, last):
                c, j = STEPS[t]
                q0 = max(0, j - PER * c) * P
                for h in range(GQ):
                    mm = pe.matmul(out[h * HD:(h + 1) * HD, q0:BANK], sta, probs[:, t % NP, h, q0:BANK],
                                   start=first, stop=last)
                return mm

            def sums(g, at):
                for t in SUMMED.get(at, []):
                    c = STEPS[t][0]
                    mine = [x for _, x in SUM_ORDER if STEPS[x][0] == c]
                    if t == mine[0]:
                        pe.wait_ge(sum_left, CH * g + c + 1)
                    into = [k for k, x in enumerate(ADDS) if ADDED[x] == t]
                    if into:
                        pe.wait_ge(add_ok, len(ADDS) * g + into[-1] + 1)
                    mm = weigh(t, sum_ps, ones[:], t == mine[0], t == mine[-1])
                return mm if SUMMED.get(at) else None

            for n, use in enumerate(ORDER[:HEAD]):
                use_bank(0, 0, n, use)
            for h in range(GQ):
                logits(0, 0, 0, h)

            def body(g, u, more):
                def max_pass(t, slot):
                    for nxt, n, use in USES.get((t, slot), []):
                        if more or not nxt:
                            use_bank(g + nxt, (u + nxt) % 2, n, use)
                def next_logits(t, h):
                    if t + 1 < NS:
                        logits(g, u, t + 1, h)
                    elif more:
                        logits(g + 1, 1 - u, 0, h)

                for t, (c, j) in enumerate(STEPS):
                    for h in range(2):
                        max_pass(t, h)
                        next_logits(t, h)
                    max_pass(t, 2)
                    sums(g, t)
                    max_pass(t, 3)
                    next_logits(t, 2)
                    max_pass(t, 4)
                    pe.wait_ge(p_ok, probs_of(g, t))
                    if j == 0:
                        pe.wait_ge(o_left, CH * g + c + 1)
                    weigh(t, o_ps, v_st[u][:, j, :], j == 0, j == PER * (c + 1) - 1).then_inc(v_ok, 1)
                    max_pass(t, 5)
                    next_logits(t, 3)
                sums(g, NS).then_inc(v_ok, 1)
            by_groups(pe, body)

        @block.vector
        def _(dve):
            dve.sem_inc(piece_used, 1)
            dve.sem_inc(o_left, 1)
            dve.sem_inc(sum_left, 1)
            dve.wait_ge(consts_in, 32)
            dve.tensor_copy(identr[:], ident[:]).then_inc(cast_ok, 1)
            dve.tensor_copy(identb[:], ident[:]).then_inc(cast_ok, 1)
            dve.tensor_copy(masks[:], masks_f[:]).then_inc(cast_ok, 1)
            dve.wait_ge(set_ok, 4)

            def max_of(g, i):
                m, at = KTILES * g + i, i % 2
                pieces = ORDER.index(("piece", i, GQ - 1, i // PER))
                pieces = sum(use[0] == "piece" for use in ORDER[:pieces + 1])

                def largest():
                    dve.wait_ge(piece_used, 2 * N_PIECES * g + 2 * pieces + 1)
                    dve.tensor_reduce(neg_max[:, at, :], mx[:, at, :, 0:i // PER + 1], AX.X, ALU.max,
                                      negate=True).then_inc(m_ok, 1)

                def high():
                    dve.wait_ge(m_ok, 2 * m + 1)
                    dve.tensor_copy(stage[:, at, :, MROW], neg_max[:, at, :]).then_inc(m_ok, 1)

                def low():
                    dve.wait_ge(m_ok, 2 * m + 2)
                    dve.tensor_tensor(stage[:, at, :, MROW + 1], neg_max[:, at, :],
                                      stage[:, at, :, MROW].bitcast(F32), ALU.subtract).then_inc(stage_ok, 1)
                return [largest, high, low]

            def take(g, n, use, chain):
                if use[0] == "turn":
                    return
                _, i, h, c = use
                dve.wait_ge(sm_ok, N_USES * g + n + 1)
                w = piece_width(use)
                dve.tensor_reduce(mx[:, i % 2, h, c:c + 1], sm[:, n % RING, 0:w], AX.X, ALU.max).then_inc(piece_used, 2)
                if chain:
                    chain.pop(0)()
                if (h, c) == (GQ - 1, i // PER):
                    chain += max_of(g, i)
                    if i == KTILES - 1:
                        while chain:
                            chain.pop(0)()

            chain = []
            for n, use in enumerate(ORDER[:HEAD]):
                take(0, n, use, chain)
            assert not chain

            def normalise(g, c):
                n = CH * g + c
                blocks = sum_t[:].rearrange("p (b k) -> p b k", k=HD)

                def turn():
                    dve.wait_ge(v_ok, N_V * (g + 1) + NP if c == CH - 1 else steps_done(g, LAST[c] + 2))
                    dve.transpose(sum_t[:], sum_ps[:]).then_inc(sum_left, 1)

                def invert():
                    dve.wait_ge(sum_left, n + 2)
                    dve.reciprocal(recip_t[:], blocks[:, :, 0]).then_inc(recip_ok, 1)

                def turn_back():
                    dve.wait_ge(recip_ok, 2 * n + 1)
                    dve.transpose(recip[:].rearrange("p (b k) -> p b k", k=HD),
                                  recip_t[:].unsqueeze(2).broadcast_to([P, BANK // HD, HD])).then_inc(recip_ok, 1)

                def scale():
                    dve.wait_ge(recip_ok, 2 * n + 2)
                    dve.wait_ge(o_left, n + 2)
                    dve.wait_ge(ol_ok, n + 1)
                    dve.tensor_tensor(o_n[:, c % 2, :], o_raw[:], recip[:], ALU.mult).then_inc(norm_ok, 1)
                return [turn, invert, turn_back, scale]

            def body(g, u, more):
                chain = []
                for t in range(NS):
                    if t - 3 in LAST:
                        norm = normalise(g, LAST.index(t - 3))
                    for slot in range(SLOTS):
                        if t - 3 in LAST and norm:
                            norm.pop(0)()
                        for nxt, n, use in USES.get((t, slot), []):
                            if more or not nxt:
                                take(g + nxt, n, use, chain)
                assert not chain
                dve.wait_ge(v_ok, steps_done(g, NS - 1))
                dve.wait_ge(norm_ok, CH * g + CH - 1)
                dve.tensor_copy(o_raw[:], o_ps[:]).then_inc(o_left, 1)
                for part in normalise(g, CH - 1):
                    part()
            by_groups(dve, body)


def output(nc, x, wo, wb, bias, w_router, lora_a, lora_b, ident_d, iota_d, o_s, out):
    with ExitStack() as ctx:
        s = Scope(nc, ctx, "p3")
        ident = s.sb("ident", [P, P], F32)
        iota = s.sb("iota", [P, EXPERTS], F32)
        bias_t = s.sb("bias", [P, HID], F32)
        wo_hi = s.sb("wo_hi", [P, KT, HID], F32R)
        wo_lo = s.sb("wo_lo", [P, KT, HID], F32R)
        wb_hi = s.sb("wb_hi", [P, KT, HID], F32R)
        wb_lo = s.sb("wb_lo", [P, KT, HID], F32R)
        ar_hi = s.sb("ar_hi", [P, KT, ARW], F32R)
        ar_lo = s.sb("ar_lo", [P, KT, ARW], F32R)
        b_t = s.sb("b_t", [P, HID], F32)
        x_t = s.sb("x", [P, 2, HID], F32)
        res = s.sb("res", [P, 2, HID], F32)
        bn = s.sb("bn", [P, 2, HID // BANK, 6], F32)
        mean_var = s.sb("mean_var", [P, 2, 2], F32)
        var_eps = s.sb("var_eps", [P, 2], F32)
        rstd = s.sb("rstd", [P, 2], F32)
        minus_half = s.sb("minus_half", [P, 1], F32)
        xt_hi = s.sb("xt_hi", [P, 2, KT, P], F32R)
        xt_lo = s.sb("xt_lo", [P, 2, KT, P], F32R)
        o_hi = s.sb("o_hi", [P, 2, KT, P], F32R)
        o_lo = s.sb("o_lo", [P, 2, KT, P], F32R)
        logit = s.sb("logit", [P, EXPERTS], F32)
        top = s.sb("top", [P, 8], F32)
        at = s.sb("at", [P, 8], U32)
        at_f = s.sb("at_f", [P, 2], F32)
        gap = s.sb("gap", [P, 1], F32)
        e_gap = s.sb("e_gap", [P, 1], F32)
        half_sum = s.sb("half_sum", [P, 1], F32)
        w_top = s.sb("w_top", [P, 2], F32)
        gate = s.sb("gate", [P, 2, EXPERTS], F32)
        gates = s.sb("gates", [P, EXPERTS], F32)
        hg = s.sb("hg", [P, ADW], F32)
        hg_t = s.sb("hg_t", [P, P], F32)
        tp = s.ps("tp", [P, KT * P])
        acc = s.ps("acc", [P, 2, HID])
        ar = s.ps("ar", [P, BANK])
        ht = s.ps("ht", [P, BANK])

        consts_in = s.sem("consts_in")
        waited = s.sem("waited")
        nat = [x_t[:, 0, :], x_t[:, 1, :], res[:, 0, :]]
        b_nat = res[:, 1, :]
        NAT = len(nat)
        w_in = [s.sem(f"w_in{k}") for k in range(NAT)]
        b_in = s.sem("b_in")
        w_tp = s.sem("w_tp")
        w_hi_ok = s.sem("w_hi_ok")
        w_lo_ok = s.sem("w_lo_ok")
        x_in = [s.sem("x_in0"), s.sem("x_in1")]
        o_in = [s.sem("o_in0"), s.sem("o_in1")]
        bn_ok = s.sem("bn_ok")
        var_ok = s.sem("var_ok")
        eps_ok = s.sem("eps_ok")
        rstd_ok = s.sem("rstd_ok")
        res_ok = s.sem("res_ok")
        xn_ok = s.sem("xn_ok")
        tp_ok = s.sem("tp_ok")
        xh_ok = s.sem("xh_ok")
        xl_ok = s.sem("xl_ok")
        ar_ok = s.sem("ar_ok")
        gap_ok = s.sem("gap_ok")
        e_ok = s.sem("e_ok")
        gate_ok = s.sem("gate_ok")
        hg_ok = s.sem("hg_ok")
        ht_ok = s.sem("ht_ok")
        hgt_ok = s.sem("hgt_ok")
        acc_ok = s.sem("acc_ok")
        out_ok = s.sem("out_ok")
        out_in = [s.sem("out_in0"), s.sem("out_in1")]
        mh_ok = s.sem("mh_ok")
        GATE_STEPS = 8

        weights = [(w[r * P:(r + 1) * P, :], P, hi[:, :, r * P:(r + 1) * P], lo[:, :, r * P:(r + 1) * P])
                   for w, hi, lo in ((wo, wo_hi, wo_lo), (wb, wb_hi, wb_lo)) for r in range(KT)]
        weights.append((lora_a.rearrange("e r d -> (e r) d"), P, ar_hi[:, :, 0:ADW], ar_lo[:, :, 0:ADW]))
        weights.append((w_router, EXPERTS, ar_hi[:, :, ADW:ARW], ar_lo[:, :, ADW:ARW]))
        NW = len(weights)

        w_ps = [tp[:], acc[:, 0, :]]

        block = ctx.enter_context(nc.Block())

        @block.sync
        def _(sp):
            sp.dma_start(ident[:], ident_d).then_inc(consts_in, 16)
            sp.dma_start(iota[:], iota_d).then_inc(consts_in, 16)
            sp.dma_start(bias_t[:], bias.partition_broadcast(P)).then_inc(consts_in, 16)
            for n, (w, rows, _, _) in enumerate(weights):
                if n == NAT:
                    for k in range(KT):
                        sp.dma_start(b_nat[:, k * P:(k + 1) * P].rearrange("p (e r) -> p e r", e=EXPERTS),
                                     lora_b[:, k * P:(k + 1) * P, :].rearrange("e o r -> o e r")
                                     ).then_inc(b_in, 16)
                if n >= NAT:
                    sp.wait_ge(w_tp, n - NAT + 1)
                sp.dma_start(nat[n % NAT][0:rows, :], w).then_inc(w_in[n % NAT], 16)

            def load(n, u):
                toks = bass.ds(n * P, P)
                if before(n, 2):
                    sp.wait_ge(w_tp, max(range(n, NW, NAT)) + 1)
                else:
                    wait_alone(sp, tp_ok, n - 1, waited)
                    sp.wait_ge(acc_ok, n - 1)
                sp.dma_start(x_t[:, u, :], x[toks, :]).then_inc(x_in[u], 16)
                for half, o in ((0, o_hi), (1, o_lo)):
                    sp.dma_start(o[:, u].bitcast(F32), o_s[half, :, toks].rearrange("(k p) t -> p k t", p=P)
                                 ).then_inc(o_in[u], 16)

            def store(n, u):
                wait_alone(sp, out_ok, n + 1, waited)
                sp.dma_start(out[bass.ds(n * P, P), :], res[:, u, :]).then_inc(out_in[u], 16)
            load(0, 0)
            load(1, 1)
            by_pairs(sp, TILES - 2, lambda n, u: (load(n + 2, u), store(n, u)))
            store(TILES - 2, 0)
            store(TILES - 1, 1)
            for u in range(2):
                sp.wait_ge(out_in[u], 16 * TILES // 2)

        @block.gpsimd
        def _(pool):
            pool.memset(minus_half[:], -0.5).then_inc(mh_ok, 1)
            pool.wait_ge(mh_ok, 1)
            pool.wait_ge(consts_in, 48)
            pool.wait_ge(w_tp, NW + 1)

            def tile(n, u):
                pool.wait_ge(x_in[u], 8 * (n - u) + 16)
                if not before(n, 2):
                    pool.wait_ge(out_in[u], 8 * (n - u))
                pool.tensor_tensor(res[:, u, :], x_t[:, u, :], bias_t[:], ALU.add).then_inc(res_ok, 1)
                wait_alone(pool, var_ok, n + 1, waited)
                pool.tensor_scalar(var_eps[:, u:u + 1], mean_var[:, u, 1:2], EPS, None, ALU.add).then_inc(eps_ok, 1)
                pool.wait_ge(eps_ok, n + 1)
                pool.tensor_tensor(rstd[:, u:u + 1], var_eps[:, u:u + 1], minus_half[:], ALU.pow).then_inc(rstd_ok, 1)
            by_pairs(pool, TILES, tile)

        @block.scalar
        def _(act):
            for n, (_, _, hi, _) in enumerate(weights):
                act.wait_ge(w_tp, n + 1)
                cols = hi.shape[2]
                act.activation(hi, w_ps[n % 2][:, 0:KT * cols].rearrange("p (k c) -> p k c", k=KT),
                               ACT.Copy).then_inc(w_hi_ok, 1)
            act.wait_ge(w_tp, NW + 1)
            act.activation(b_t[:], tp[:], ACT.Copy).then_inc(w_hi_ok, 1)

            def x_hi(n, u):
                act.wait_ge(tp_ok, n + 1)
                if not before(n, 2):
                    act.wait_ge(acc_ok, n - 1)
                act.activation(xt_hi[:, u].rearrange("p k c -> p (k c)"), tp[:], ACT.Copy).then_inc(xh_ok, 1)

            x_hi(0, 0)

            def tile(n, u):
                act.wait_ge(gap_ok, n + 1)
                act.activation(e_gap[:], gap[:], ACT.Exp).then_inc(e_ok, 1)
                if not (isinstance(n, int) and n == TILES - 1):
                    x_hi(n + 1, 1 - u)
                act.wait_ge(ht_ok, n + 1)
                if not before(n, 1):
                    act.wait_ge(acc_ok, n)
                act.activation(hg_t[:], ht[:, 0:P], ACT.Copy).then_inc(hgt_ok, 1)
            by_pairs(act, TILES, tile)

        @block.tensor
        def _(pe):
            pe.wait_ge(consts_in, 48)
            for n, (_, rows, hi, _) in enumerate(weights):
                pe.wait_ge(w_in[n % NAT], 16 * (n // NAT + 1))
                if n >= 2:
                    pe.wait_ge(w_hi_ok, n - 1)
                    pe.wait_ge(w_lo_ok, n - 1)
                for k in range(KT):
                    mm = pe.transpose(w_ps[n % 2][:, k * rows:(k + 1) * rows], nat[n % NAT][0:rows, k * P:(k + 1) * P],
                                      ident[0:rows, 0:rows])
                mm.then_inc(w_tp, 1)
            pe.wait_ge(b_in, 16 * KT)
            pe.wait_ge(w_hi_ok, NW)
            pe.wait_ge(w_lo_ok, NW)
            for k in range(KT):
                mm = pe.transpose(tp[:, k * P:(k + 1) * P], b_nat[:, k * P:(k + 1) * P], ident[:])
            mm.then_inc(w_tp, 1)

            def turn_x(n, u):
                pe.wait_ge(xn_ok, n + 1)
                if before(n, 1):
                    pe.wait_ge(w_hi_ok, NW + 1)
                else:
                    pe.wait_ge(xh_ok, n)
                    pe.wait_ge(xl_ok, n)
                for k in range(KT):
                    mm = pe.transpose(tp[:, k * P:(k + 1) * P], x_t[:, u, k * P:(k + 1) * P], ident[:])
                mm.then_inc(tp_ok, 1)

            def half_products(n, u, c):
                cols = slice(c * BANK, (c + 1) * BANK)
                for k in range(KT):
                    three_passes(pe, acc[:, u, cols], o_hi[:, u, k, :], o_lo[:, u, k, :],
                                 wo_hi[:, k, cols], wo_lo[:, k, cols], k == 0, False)
                for k in range(KT):
                    three_passes(pe, acc[:, u, cols], xt_hi[:, u, k, :], xt_lo[:, u, k, :],
                                 wb_hi[:, k, cols], wb_lo[:, k, cols], False, False)

            turn_x(0, 0)

            def tile(n, u):
                pe.wait_ge(xh_ok, n + 1)
                pe.wait_ge(xl_ok, n + 1)
                if not before(n, 1):
                    pe.wait_ge(hg_ok, n)
                for k in range(KT):
                    mm = three_passes(pe, ar[:, 0:ARW], xt_hi[:, u, k, :], xt_lo[:, u, k, :],
                                      ar_hi[:, k, :], ar_lo[:, k, :], k == 0, k == KT - 1)
                mm.then_inc(ar_ok, 1)
                pe.wait_ge(o_in[u], 16 * (n - u) + 32)
                if not before(n, 2):
                    pe.wait_ge(out_ok, n - 1)
                half_products(n, u, 0)
                if not (isinstance(n, int) and n == TILES - 1):
                    turn_x(n + 1, 1 - u)
                pe.wait_ge(hg_ok, n + 1)
                if not before(n, 1):
                    pe.wait_ge(hgt_ok, n)
                pe.transpose(ht[:, 0:P], hg[:], ident[:]).then_inc(ht_ok, 1)
                half_products(n, u, 1)
                pe.wait_ge(hgt_ok, n + 1)
                for c in range(HID // BANK):
                    cols = slice(c * BANK, (c + 1) * BANK)
                    mm = pe.matmul(acc[:, u, cols], hg_t[:], b_t[:, cols], start=False, stop=True)
                mm.then_inc(acc_ok, 1)
            by_pairs(pe, TILES, tile)

        @block.vector
        def _(dve):
            dve.wait_ge(consts_in, 48)
            for n, (_, _, hi, lo) in enumerate(weights):
                cols = hi.shape[2]
                dve.wait_ge(w_hi_ok, n + 1)
                dve.tensor_tensor(lo, w_ps[n % 2][:, 0:KT * cols].rearrange("p (k c) -> p k c", k=KT),
                                  hi.bitcast(F32), ALU.subtract).then_inc(w_lo_ok, 1)

            def normalise(n, u):
                dve.wait_ge(x_in[u], 8 * (n - u) + 16)
                for c in range(HID // BANK):
                    dve.bn_stats(bn[:, u, c, :], x_t[:, u, c * BANK:(c + 1) * BANK]).then_inc(bn_ok, 1)
                wait_alone(dve, bn_ok, 2 * n + 2, waited)
                dve.bn_aggr(mean_var[:, u, :], bn[:, u].rearrange("p c s -> p (c s)")).then_inc(var_ok, 1)
                dve.wait_ge(var_ok, n + 1)
                dve.wait_ge(rstd_ok, n + 1)
                dve.wait_ge(res_ok, n + 1)
                dve.tensor_scalar(x_t[:, u, :], x_t[:, u, :], mean_var[:, u, 0:1], rstd[:, u:u + 1],
                                  ALU.subtract, ALU.mult).then_inc(xn_ok, 1)

            def x_lo(n, u):
                dve.wait_ge(xh_ok, n + 1)
                dve.tensor_tensor(xt_lo[:, u].rearrange("p k c -> p (k c)"), tp[:],
                                  xt_hi[:, u].rearrange("p k c -> p (k c)").bitcast(F32),
                                  ALU.subtract).then_inc(xl_ok, 1)

            def route(n):
                step = 0

                def then(ins):
                    nonlocal step
                    step += 1
                    ins.then_inc(gate_ok, 1)
                    wait_alone(dve, gate_ok, GATE_STEPS * n + step, waited)
                dve.wait_ge(ar_ok, n + 1)
                then(dve.tensor_copy(logit[:], ar[:, ADW:ARW]))
                then(dve.max(out=top[:], in_=logit[:]))
                dve.tensor_tensor(gap[:], top[:, 1:2], top[:, 0:1], ALU.subtract).then_inc(gap_ok, 1)
                then(dve.max_index(out=at[:], in_max=top[:], in_values=logit[:]))
                dve.tensor_copy(at_f[:], at[:, 0:2])
                dve.wait_ge(e_ok, n + 1)
                then(dve.tensor_scalar(half_sum[:], e_gap[:], 1.0, 1.0 / LORA_SCALE, ALU.add, ALU.mult))
                then(dve.reciprocal(w_top[:, 0:1], half_sum[:]))
                then(dve.tensor_tensor(w_top[:, 1:2], w_top[:, 0:1], e_gap[:], ALU.mult))
                for k in range(2):
                    ins = dve.tensor_scalar(gate[:, k, :], iota[:], at_f[:, k:k + 1], w_top[:, k:k + 1],
                                            ALU.is_equal, ALU.mult)
                then(ins)
                then(dve.tensor_tensor(gates[:], gate[:, 0, :], gate[:, 1, :], ALU.add))
                dve.tensor_tensor(hg[:].rearrange("p (e r) -> p e r", e=EXPERTS),
                                  ar[:, 0:ADW].rearrange("p (e r) -> p e r", e=EXPERTS),
                                  gates[:].unsqueeze(2).broadcast_to([P, EXPERTS, RANK]),
                                  ALU.mult).then_inc(hg_ok, 1)
                assert step == GATE_STEPS

            def finish(n, u):
                dve.wait_ge(acc_ok, n + 1)
                dve.tensor_tensor(res[:, u, :], acc[:, u, :], res[:, u, :], ALU.add).then_inc(out_ok, 1)

            normalise(0, 0)
            x_lo(0, 0)

            def tile(n, u):
                if not before(n, 1):
                    finish(n - 1, 1 - u)
                route(n)
                if not (isinstance(n, int) and n == TILES - 1):
                    normalise(n + 1, 1 - u)
                    x_lo(n + 1, 1 - u)
            by_pairs(dve, TILES, tile)
            finish(TILES - 1, 1)


def build(nc, ins, out):
    def scratch(name, shape):
        return nc.dram_tensor(name, shape, F32, kind="Internal").ap()
    q_s = scratch("q_halves", [2, HID, TOKENS])
    k_s = scratch("k_halves", [2, KVW, TOKENS])
    v_s = scratch("v_rows", [TOKENS, KVW])
    o_s = scratch("o_halves", [2, HID, TOKENS])
    x = ins["L0_attn_hidden_states"].rearrange("b s d -> (b s) d")
    project_qkv(nc, x, ins["L0_attn_Wq"], ins["L0_attn_Wk"], ins["L0_attn_Wv"], ins["rope"], ins["ident"],
                q_s, k_s, v_s)
    attention(nc, q_s, k_s, v_s, ins["ident"], ins["masks"], o_s)
    output(nc, x, ins["L0_attn_Wo"], ins["L0_ffn_W_base"], ins["L0_ffn_b_base"], ins["L0_ffn_W_router"],
           ins["L0_ffn_lora_A"], ins["L0_ffn_lora_B"], ins["ident"], ins["iota"], o_s,
           out.rearrange("b s d -> (b s) d"))


def constants():
    import numpy as np

    inv_freq = (1.0 / np.float32(10000.0) ** (np.arange(0, HD, 2, dtype=np.float32) / np.float32(HD))).astype(np.float32)
    angle = np.outer(np.arange(SEQ, dtype=np.float32), inv_freq).astype(np.float32)
    cos, sin = np.cos(angle), np.sin(angle)
    row = np.concatenate([cos, cos, -sin, sin], axis=1).astype(np.float32)
    order = np.arange(P)
    hidden = np.where(order[None, :] <= order[:, None], 0.0, -1e30)
    return {
        "rope": np.ascontiguousarray(np.tile(row, (BATCH, 1)).reshape(TILES, P, 2 * HD).transpose(1, 0, 2)),
        "ident": np.eye(P, dtype=np.float32),
        "masks": np.stack([hidden, hidden.T], axis=1).astype(np.float32),
        "iota": np.tile(np.arange(EXPERTS, dtype=np.float32), (P, 1)),
    }


def kernel(**inputs):
    import numpy as np
    import concourse.bacc as bacc
    from concourse.bass_utils import run_bass_kernel_spmd

    nc = bacc.Bacc("TRN2", target_bir_lowering=False, num_devices=1)
    arrays, ins = {}, {}
    for name, value in {**inputs, **constants()}.items():
        a = np.ascontiguousarray(value)
        arrays[f"in_{name}"] = a
        ins[name] = nc.dram_tensor(f"in_{name}", a.shape, mybir.dt.from_np(a.dtype), kind="ExternalInput").ap()
    out = nc.dram_tensor("out_dram", (BATCH, SEQ, HID), F32, kind="ExternalOutput").ap()
    build(nc, ins, out)
    r = run_bass_kernel_spmd(nc, [arrays], core_ids=[0])
    return r.results[0]["out_dram"]
```

```python
from contextlib import ExitStack

import concourse.bass as bass
from concourse import mybir

F32 = mybir.dt.float32
F32R = mybir.dt.float32r
BF16 = mybir.dt.bfloat16
U32 = mybir.dt.uint32
ALU = mybir.AluOpType
ACT = mybir.ActivationFunctionType
AX = mybir.AxisListType

P = 128
BATCH, SEQ, HID = 2, 2048, 1024
NH, NKV, HD = 32, 8, 32
GQ = NH // NKV
HALF = HD // 2
EXPERTS, RANK = 8, 16
TOKENS = BATCH * SEQ
TILES = TOKENS // P
KT = HID // P
KVW = NKV * HD
QKVW = HID + 2 * KVW
BANK = 512
QKH = NH + NKV
FT = QKH * HD // P
GROUPS = BATCH * NKV
CH = SEQ // BANK
KTILES = SEQ // P
PER = BANK // P
EPS = 1e-5
SM_SCALE = float(HD) ** -0.5
LORA_SCALE = 2.0
MROW = 3 * HD
KROWS = MROW + 2
ADW = EXPERTS * RANK
ARW = ADW + EXPERTS
REST = 3 * P
FIRST = HID - 2 * REST


class Scope:

    def __init__(self, nc, ctx, tag):
        self.nc, self.ctx, self.tag = nc, ctx, tag

    def sb(self, name, shape, dtype):
        return self.ctx.enter_context(self.nc.sbuf_tensor(f"{self.tag}_{name}", shape, dtype))

    def ps(self, name, shape, dtype=F32):
        return self.ctx.enter_context(self.nc.psum_tensor(f"{self.tag}_{name}", shape, dtype))

    def sem(self, name):
        return self.ctx.enter_context(self.nc.semaphore(f"{self.tag}_{name}"))


def by_pairs(eng, count, tile):
    tile(0, 0)
    tile(1, 1)
    with eng.Fori(1, count // 2 - 1) as i:
        tile(2 * i, 0)
        tile(2 * i + 1, 1)
    tile(count - 2, 0)
    tile(count - 1, 1)


def before(n, k):
    return isinstance(n, int) and n < k


def wait_alone(eng, sem, value, waited):
    eng.wait_ge(sem, value)
    eng.sem_inc(waited, 1)


def three_passes(pe, out, sta_hi, sta_lo, mov_hi, mov_lo, first, last):
    pe.matmul(out, sta_hi, mov_hi, start=first, stop=False)
    pe.matmul(out, sta_hi, mov_lo, start=False, stop=False)
    return pe.matmul(out, sta_lo, mov_hi, start=False, stop=last)


def project_qkv(nc, x, wq, wk, wv, rope, ident_d, q_s, k_s, v_s):
    with ExitStack() as ctx:
        s = Scope(nc, ctx, "p1")
        NAT = 4
        ident = s.sb("ident", [P, P], F32)
        w_nat = s.sb("w_nat", [P, NAT, HID], F32)
        w_hi = s.sb("w_hi", [P, KT, QKVW], F32R)
        w_lo = s.sb("w_lo", [P, KT, QKVW], F32R)
        x_t = s.sb("x", [P, 2, HID], F32)
        rope_t = s.sb("rope", [P, TILES, 2 * HD], F32)
        bn = s.sb("bn", [P, 2, HID // BANK, 6], F32)
        mean_var = s.sb("mean_var", [P, 2, 2], F32)
        var_eps = s.sb("var_eps", [P, 2], F32)
        rstd = s.sb("rstd", [P, 2], F32)
        minus_half = s.sb("minus_half", [P, 1], F32)
        xt_hi = s.sb("xt_hi", [P, 2, KT, P], F32R)
        xt_lo = s.sb("xt_lo", [P, 2, KT, P], F32R)
        by_cos = s.sb("by_cos", [P, QKH, HD], F32)
        by_sin = s.sb("by_sin", [P, QKH, HD], F32)
        rot = s.sb("rot", [P, QKH * HD], F32)
        v_t = s.sb("v", [P, 2, KVW], F32)
        f_hi = s.sb("f_hi", [P, FT, P], F32R)
        f_lo = s.sb("f_lo", [P, FT, P], F32R)
        tp = s.ps("tp", [P, KT * P])
        qkv = s.ps("qkv", [P, QKVW])
        ft = s.ps("ft", [P, 3 * BANK])

        consts_in = s.sem("consts_in")
        waited = s.sem("waited")
        w_in = [s.sem(f"w_in{k}") for k in range(NAT)]
        w_tp = s.sem("w_tp")
        w_hi_ok = s.sem("w_hi_ok")
        w_lo_ok = s.sem("w_lo_ok")
        rope_in = s.sem("rope_in")
        x_in = [s.sem("x_in0"), s.sem("x_in1")]
        bn_ok = s.sem("bn_ok")
        agg_ok = s.sem("agg_ok")
        eps_ok = s.sem("eps_ok")
        rstd_ok = s.sem("rstd_ok")
        xn_ok = s.sem("xn_ok")
        tp_ok = s.sem("tp_ok")
        xh_ok = s.sem("xh_ok")
        xl_ok = s.sem("xl_ok")
        mm_ok = s.sem("mm_ok")
        cs_ok = s.sem("cs_ok")
        v_ok = s.sem("v_ok")
        rot_ok = s.sem("rot_ok")
        ft_ok = s.sem("ft_ok")
        fh_ok = s.sem("fh_ok")
        fl_ok = s.sem("fl_ok")
        f_out = s.sem("f_out")
        v_out = [s.sem("v_out0"), s.sem("v_out1")]
        mh_ok = s.sem("mh_ok")

        weights = [(wq, r, r * P) for r in range(HID // P)]
        weights += [(wk, r, HID + r * P) for r in range(KVW // P)]
        weights += [(wv, r, HID + KVW + r * P) for r in range(KVW // P)]
        NW = len(weights)
        BANKS = QKVW // BANK
        heads_in = [(c * BANK // HD, min((c + 1) * BANK // HD, QKH)) for c in range(BANKS)]

        w_ps = [tp[:], qkv[:, 0:KT * P], ft[:, 0:KT * P]]
        WPS = len(w_ps)

        block = ctx.enter_context(nc.Block())

        @block.sync
        def _(sp):
            sp.dma_start(ident[:], ident_d).then_inc(consts_in, 16)

            def load(n, u):
                if not before(n, 2):
                    wait_alone(sp, tp_ok, n - 1, waited)
                sp.dma_start(x_t[:, u, :], x[bass.ds(n * P, P), :]).then_inc(x_in[u], 16)

            for n, (w, r, _) in enumerate(weights):
                if n >= NAT:
                    sp.wait_ge(w_tp, n - NAT + 1)
                sp.dma_start(w_nat[:, n % NAT, :], w[r * P:(r + 1) * P, :]).then_inc(w_in[n % NAT], 16)
                if n == NAT - 1:
                    load(0, 0)
            sp.dma_start(rope_t[:], rope).then_inc(rope_in, 16)
            load(1, 1)

            def store(n, u):
                toks = bass.ds(n * P, P)
                wait_alone(sp, v_ok, n + 1, waited)
                sp.dma_start(v_s[toks, :], v_t[:, u, :]).then_inc(v_out[u], 16)
                for half, f, ready in ((0, f_hi, fh_ok), (1, f_lo, fl_ok)):
                    wait_alone(sp, ready, n + 1, waited)
                    sp.dma_start(q_s[half, :, toks].rearrange("(f p) t -> p f t", p=P),
                                 f[:, 0:HID // P, :].bitcast(F32)).then_inc(f_out, 16)
                    sp.dma_start(k_s[half, :, toks].rearrange("(f p) t -> p f t", p=P),
                                 f[:, HID // P:FT, :].bitcast(F32)).then_inc(f_out, 16)

            load(2, 0)
            by_pairs(sp, TILES - 4, lambda n, u: (load(n + 3, 1 - u), store(n, u)))
            load(TILES - 1, 1)
            for n in range(TILES - 4, TILES):
                store(n, n % 2)
            sp.wait_ge(f_out, 64 * TILES)
            for u in range(2):
                sp.wait_ge(v_out[u], 16 * TILES // 2)

        @block.gpsimd
        def _(pool):
            pool.memset(minus_half[:], -0.5).then_inc(mh_ok, 1)
            pool.wait_ge(mh_ok, 1)

            def rstd_of(n, u):
                wait_alone(pool, agg_ok, n + 1, waited)
                pool.tensor_scalar(var_eps[:, u:u + 1], mean_var[:, u, 1:2], EPS, None, ALU.add).then_inc(eps_ok, 1)
                pool.wait_ge(eps_ok, n + 1)
                pool.tensor_tensor(rstd[:, u:u + 1], var_eps[:, u:u + 1], minus_half[:], ALU.pow).then_inc(rstd_ok, 1)

            def rotate(n, u):
                pool.wait_ge(cs_ok, BANKS * (n + 1))
                if not before(n, 1):
                    pool.wait_ge(ft_ok, n)
                pool.tensor_tensor(rot[:], by_cos[:].rearrange("p h d -> p (h d)"),
                                   by_sin[:].rearrange("p h d -> p (h d)"), ALU.add).then_inc(rot_ok, 1)

            rstd_of(0, 0)

            def tile(n, u):
                if not (isinstance(n, int) and n == TILES - 1):
                    rstd_of(n + 1, 1 - u)
                rotate(n, u)
            by_pairs(pool, TILES, tile)

        @block.scalar
        def _(act):
            for n, (_, _, col) in enumerate(weights):
                act.wait_ge(w_tp, n + 1)
                act.activation(w_hi[:, :, col:col + P], w_ps[n % WPS].rearrange("p (k c) -> p k c", k=KT),
                               ACT.Copy).then_inc(w_hi_ok, 1)

            def x_hi(n, u):
                act.wait_ge(tp_ok, n + 1)
                if not before(n, 2):
                    act.wait_ge(mm_ok, BANKS * (n - 1))
                act.activation(xt_hi[:, u].rearrange("p k c -> p (k c)"), tp[:], ACT.Copy).then_inc(xh_ok, 1)

            def v_copy(n, u):
                act.wait_ge(cs_ok, BANKS * (n + 1))
                if not before(n, 2):
                    act.wait_ge(v_out[u], 8 * (n - u))
                act.activation(v_t[:, u, :], qkv[:, HID + KVW:QKVW], ACT.Copy).then_inc(v_ok, 1)

            def f_hi_copy(n):
                act.wait_ge(ft_ok, n + 1)
                if not before(n, 1):
                    act.wait_ge(f_out, 64 * n)
                act.activation(f_hi[:].rearrange("p f c -> p (f c)"), ft[:, 0:FT * P], ACT.Copy).then_inc(fh_ok, 1)

            x_hi(0, 0)

            def tile(n, u):
                if not before(n, 1):
                    f_hi_copy(n - 1)
                if not (isinstance(n, int) and n == TILES - 1):
                    x_hi(n + 1, 1 - u)
                v_copy(n, u)
            by_pairs(act, TILES, tile)
            f_hi_copy(TILES - 1)

        @block.tensor
        def _(pe):
            pe.wait_ge(consts_in, 16)
            for n in range(NW):
                pe.wait_ge(w_in[n % NAT], 16 * (n // NAT + 1))
                if n >= WPS:
                    pe.wait_ge(w_hi_ok, n - WPS + 1)
                    pe.wait_ge(w_lo_ok, n - WPS + 1)
                for k in range(KT):
                    mm = pe.transpose(w_ps[n % WPS][:, k * P:(k + 1) * P], w_nat[:, n % NAT, k * P:(k + 1) * P], ident[:])
                mm.then_inc(w_tp, 1)

            def turn_x(n, u):
                pe.wait_ge(xn_ok, n + 1)
                if before(n, 1):
                    pe.wait_ge(w_hi_ok, NW)
                    pe.wait_ge(w_lo_ok, NW)
                else:
                    pe.wait_ge(xh_ok, n)
                    pe.wait_ge(xl_ok, n)
                for k in range(KT):
                    mm = pe.transpose(tp[:, k * P:(k + 1) * P], x_t[:, u, k * P:(k + 1) * P], ident[:])
                mm.then_inc(tp_ok, 1)

            def products(n, u, c):
                if c == 0:
                    pe.wait_ge(xh_ok, n + 1)
                    pe.wait_ge(xl_ok, n + 1)
                if not before(n, 1):
                    pe.wait_ge(cs_ok, BANKS * (n - 1) + c + 1)
                    if c == BANKS - 1:
                        pe.wait_ge(v_ok, n)
                cols = slice(c * BANK, (c + 1) * BANK)
                for k in range(KT):
                    mm = three_passes(pe, qkv[:, cols], xt_hi[:, u, k, :], xt_lo[:, u, k, :],
                                      w_hi[:, k, cols], w_lo[:, k, cols], k == 0, k == KT - 1)
                mm.then_inc(mm_ok, 1)

            def turn_f(n):
                pe.wait_ge(rot_ok, n + 1)
                if not before(n, 1):
                    pe.wait_ge(fh_ok, n)
                    pe.wait_ge(fl_ok, n)
                for f in range(FT):
                    mm = pe.transpose(ft[:, f * P:(f + 1) * P], rot[:, f * P:(f + 1) * P], ident[:])
                mm.then_inc(ft_ok, 1)

            turn_x(0, 0)

            def tile(n, u):
                products(n, u, 0)
                if not before(n, 1):
                    turn_f(n - 1)
                products(n, u, 1)
                if not (isinstance(n, int) and n == TILES - 1):
                    turn_x(n + 1, 1 - u)
                products(n, u, 2)
            by_pairs(pe, TILES, tile)
            turn_f(TILES - 1)

        @block.vector
        def _(dve):
            def split_weights(n):
                col = weights[n][2]
                dve.wait_ge(w_hi_ok, n + 1)
                dve.tensor_tensor(w_lo[:, :, col:col + P], w_ps[n % WPS].rearrange("p (k c) -> p k c", k=KT),
                                  w_hi[:, :, col:col + P].bitcast(F32), ALU.subtract).then_inc(w_lo_ok, 1)

            def normalise(n, u):
                dve.wait_ge(x_in[u], 8 * (n - u) + 16)
                for c in range(HID // BANK):
                    dve.bn_stats(bn[:, u, c, :], x_t[:, u, c * BANK:(c + 1) * BANK]).then_inc(bn_ok, 1)
                wait_alone(dve, bn_ok, 2 * n + 2, waited)
                dve.bn_aggr(mean_var[:, u, :], bn[:, u].rearrange("p c s -> p (c s)")).then_inc(agg_ok, 1)
                dve.wait_ge(agg_ok, n + 1)
                dve.wait_ge(rstd_ok, n + 1)
                dve.tensor_scalar(x_t[:, u, :], x_t[:, u, :], mean_var[:, u, 0:1], rstd[:, u:u + 1],
                                  ALU.subtract, ALU.mult).then_inc(xn_ok, 1)

            def x_lo(n, u):
                dve.wait_ge(xh_ok, n + 1)
                dve.tensor_tensor(xt_lo[:, u].rearrange("p k c -> p (k c)"), tp[:],
                                  xt_hi[:, u].rearrange("p k c -> p (k c)").bitcast(F32),
                                  ALU.subtract).then_inc(xl_ok, 1)

            def rotary(n, u, c):
                h0, h1 = heads_in[c]
                dve.wait_ge(mm_ok, BANKS * n + c + 1)
                if c == 0 and not before(n, 1):
                    dve.wait_ge(rot_ok, n)
                q = qkv[:, h0 * HD:h1 * HD].rearrange("p (h d) -> p h d", d=HD)
                table = rope_t[:, bass.ds(n, 1), :]
                wide = lambda a, b: table[:, :, a:b].broadcast_to([P, h1 - h0, b - a])
                dve.tensor_tensor(by_cos[:, h0:h1, :], q, wide(0, HD), ALU.mult)
                dve.tensor_tensor(by_sin[:, h0:h1, 0:HALF], q[:, :, HALF:HD], wide(HD, HD + HALF), ALU.mult)
                dve.tensor_tensor(by_sin[:, h0:h1, HALF:HD], q[:, :, 0:HALF], wide(HD + HALF, 2 * HD),
                                  ALU.mult).then_inc(cs_ok, 1)

            def f_lo_sub(n):
                dve.wait_ge(fh_ok, n + 1)
                dve.tensor_tensor(f_lo[:].rearrange("p f c -> p (f c)"), ft[:, 0:FT * P],
                                  f_hi[:].rearrange("p f c -> p (f c)").bitcast(F32), ALU.subtract).then_inc(fl_ok, 1)

            for n in range(NW):
                if n == NW - 2:
                    normalise(0, 0)
                split_weights(n)
            x_lo(0, 0)
            dve.wait_ge(rope_in, 16)

            def tile(n, u):
                if not (isinstance(n, int) and n == TILES - 1):
                    normalise(n + 1, 1 - u)
                rotary(n, u, 0)
                if not before(n, 1):
                    f_lo_sub(n - 1)
                rotary(n, u, 1)
                if not (isinstance(n, int) and n == TILES - 1):
                    x_lo(n + 1, 1 - u)
                rotary(n, u, 2)
            by_pairs(dve, TILES, tile)
            f_lo_sub(TILES - 1)


STEPS = [(c, j) for c in range(CH) for j in range(PER * (c + 1))]
NS = len(STEPS)
LAST = [STEPS.index((c, PER * (c + 1) - 1)) for c in range(CH)]
SLOTS = 6
RING = 3
HEADS = GQ * NS
CHAIN = 6
AHEAD = 11
NP = 8


COL, VEC_COL, ACT_COL, VEC_FIXED, ACT_FIXED, HOP, NORM = 1 / 2.4, 1.04, 0.83, 65, 60, 80, 600
EARLY, FILLER, LATE = 700, 2000, 3000


def max_order():
    uses, due = [], []
    for i in range(KTILES):
        for h in range(GQ):
            for c in range(i // PER + 1):
                uses.append(("piece", i, h, c))
                if due and due[0][0] == len(uses):
                    uses.append(("turn", due.pop(0)[1]))
        due.append((len(uses) + CHAIN, i))
    assert len(due) == 1
    return uses + [("turn", KTILES - 1)]


ORDER = max_order()
N_USES = len(ORDER)
N_PIECES = sum(use[0] == "piece" for use in ORDER)
HEAD = ORDER.index(("turn", AHEAD - 1)) + 1


def freed(n):
    if n < RING:
        return ORDER[max(range(n, N_USES, RING))][0], 0
    kind = ORDER[n - RING][0]
    return kind, sum(use[0] == kind for use in ORDER[:n - RING + 1])


def head_bank(k):
    return (k + HEADS) % RING if k < RING else k % RING


def head_freed(k):
    before_it = [x for x in range(k) if head_bank(x) == head_bank(k)]
    return before_it[-1] + 1 if before_it else k - RING + 1


def piece_width(use):
    _, i, _, c = use
    return (i % PER + 1) * P if c == i // PER else BANK


def max_schedule():
    uses = [(0, n, ORDER[n]) for n in range(HEAD, N_USES)] + [(1, n, ORDER[n]) for n in range(HEAD)]
    slots = [(t, slot) for t in range(NS) for slot in range(SLOTS)]
    width = [BANK - max(0, j - PER * c) * P for c, j in STEPS]

    def vector_work(use):
        return piece_width(use) * VEC_COL + VEC_FIXED if use[0] == "piece" else 0

    def tensor_work(t, slot):
        if slot in (2, 4):
            return GQ * COL * (width[t] if slot == 4 else sum(width[x] for x in SUMMED.get(t, [])))
        return width[(t + 1) % NS] * COL

    todo, total = sum(vector_work(use) for _, _, use in uses), sum(tensor_work(*x) for x in slots)
    tensor = scalar = vector = done = passed = 0
    free = {HEAD - k: 0 for k in range(1, RING + 1)}
    exp = [0] * (HEADS + GQ)
    staged, schedule, k = {}, {}, HEAD
    for x in slots:
        t, slot = x
        head = GQ * (t + 1) + {0: 0, 1: 1, 3: 2, 5: 3}.get(slot, 0)
        needs = {2: 0, 4: exp[GQ * t + 3]}.get(slot, exp[head - RING])
        if t - 3 in LAST and slot < 4:
            vector = max(vector, tensor) + NORM
        while uses:
            use = uses[0][2]
            work = vector_work(use)
            late = todo * passed / total - done - work
            ready = max(free[k - RING], staged.get(use[1], 0) if use[0] == "turn" else 0)
            waits = needs > tensor + VEC_FIXED
            if x != slots[-1] and (late < -(FILLER if waits else EARLY) or
                                   (ready > (needs if waits else tensor) and late < LATE)):
                break
            tensor = max(tensor, ready)
            if use[0] == "piece":
                tensor += piece_width(use) * COL
                vector = max(vector, tensor + HOP) + work
                free[k] = vector + HOP
                if use[2] == GQ - 1 and use[3] == use[1] // PER:
                    staged[use[1]] = vector + 3 * 2 * VEC_FIXED
                    vector += 3 * VEC_FIXED
            else:
                tensor += BANK * COL
                scalar = max(scalar, tensor + HOP) + BANK * ACT_COL + ACT_FIXED
                free[k] = scalar + HOP
            done += work
            k += 1
            schedule.setdefault(x, []).append(uses.pop(0))
        tensor = max(tensor, needs) + tensor_work(t, slot)
        passed += tensor_work(t, slot)
        if slot not in (2, 4):
            scalar = max(scalar, tensor + HOP) + width[(t + 1) % NS] * ACT_COL + ACT_FIXED
            exp[head] = scalar + HOP
    assert not uses
    for (t, _), here in schedule.items():
        for nxt, _, use in here:
            if use[0] == "turn" and nxt == 0:
                assert t + 1 < STEPS.index((use[1] // PER, 0)), "turned in time for its chunk"
    return schedule


def sum_schedule():
    added, summed = {}, {}
    for c in range(CH):
        for j in range(0, PER * (c + 1), PER):
            t = STEPS.index((c, j))
            if c == CH - 1 and j == PER * c:
                for k in range(PER):
                    summed.setdefault(t + k + 1, []).append(t + k)
                continue
            whole = j < PER * c
            for k in range(1, PER):
                added[t + k] = t
            summed.setdefault(t + 5 + whole, []).append(t)
    return added, summed


ADDED, SUMMED = sum_schedule()
USES = max_schedule()
SUM_ORDER = [(n, x) for n in sorted(SUMMED) for x in SUMMED[n]]
ADDS = sorted(ADDED)
N_V = NS + 1
LOADS = 7


def attention(nc, q_s, k_s, v_s, ident_d, mask_d, o_s):
    with ExitStack() as ctx:
        s = Scope(nc, ctx, "p2")
        ident = s.sb("ident", [P, P], F32)
        identr = s.sb("identr", [P, P], F32R)
        identb = s.sb("identb", [P, P], BF16)
        masks_f = s.sb("masks_f", [P, 2, P], F32)
        masks = s.sb("masks", [P, 2, P], BF16)
        ones = s.sb("ones", [P, HD], F32)
        q_st = [s.sb(f"q_st{u}", [P, GQ, SEQ], F32R) for u in range(2)]
        k_st = [s.sb(f"k_st{u}", [P, SEQ], F32R) for u in range(2)]
        v_st = [s.sb(f"v_st{u}", [P, KTILES, HD], F32) for u in range(2)]
        probs = s.sb("probs", [P, NP, GQ, BANK], F32)
        mx = s.sb("mx", [P, 2, GQ, CH], F32)
        neg_max = s.sb("neg_max", [P, 2, GQ], F32)
        stage = s.sb("stage", [P, 2, GQ, KROWS], F32R)
        o_raw = s.sb("o_raw", [P, BANK], F32)
        sum_t = s.sb("sum_t", [P, BANK], F32)
        recip_t = s.sb("recip_t", [P, BANK // HD], F32)
        recip = s.sb("recip", [P, BANK], F32)
        o_n = s.sb("o_n", [P, 2, BANK], F32)
        o_hi = s.sb("o_hi", [P, 2, BANK], F32R)
        o_lo = s.sb("o_lo", [P, 2, BANK], F32R)
        st = s.ps("st", [P, RING, BANK])
        sm = s.ps("sm", [P, RING, BANK])
        o_ps = s.ps("o", [P, BANK])
        sum_ps = s.ps("sum", [P, BANK])

        consts_in = s.sem("consts_in")
        waited = s.sem("waited")
        set_ok = s.sem("set_ok")
        cast_ok = s.sem("cast_ok")
        loaded = [[s.sem(f"loaded{u}{c}") for c in range(CH)] for u in range(2)]
        sm_ok = s.sem("sm_ok")
        piece_used = s.sem("piece_used")
        turn_used = s.sem("turn_used")
        m_ok = s.sem("m_ok")
        stage_ok = s.sem("stage_ok")
        st_ok = s.sem("st_ok")
        p_ok = s.sem("p_ok")
        v_ok = s.sem("v_ok")
        add_ok = s.sem("add_ok")
        o_left = s.sem("o_left")
        sum_left = s.sem("sum_left")
        recip_ok = s.sem("recip_ok")
        norm_ok = s.sem("norm_ok")
        oh_ok = s.sem("oh_ok")
        ol_ok = s.sem("ol_ok")
        o_out = [s.sem("o_out0"), s.sem("o_out1")]

        def by_groups(eng, body):
            with eng.Fori(0, GROUPS // 2 - 1) as i:
                body(2 * i, 0, True)
                body(2 * i + 1, 1, True)
            body(GROUPS - 2, 0, True)
            body(GROUPS - 1, 1, False)

        def probs_of(g, t):
            return HEADS * g + GQ * (t + 1) + RING

        def steps_done(g, t):
            return N_V * g + t + 1 + NP

        block = ctx.enter_context(nc.Block())

        @block.sync
        def _(sp):
            sp.dma_start(ident[:], ident_d).then_inc(consts_in, 16)
            sp.dma_start(masks_f[:], mask_d).then_inc(consts_in, 16)

            def load(g, u):
                for c in range(CH):
                    cols = slice(c * BANK, (c + 1) * BANK)
                    batch, kv = g // NKV, g % NKV
                    toks = bass.ds(batch * SEQ + c * BANK, BANK)
                    for row, half in ((0, 0), (HD, 0), (2 * HD, 1)):
                        src = q_s[half, bass.ds(kv * P, P), toks].rearrange("(h d) t -> d h t", d=HD)
                        sp.dma_start(q_st[u][row:row + HD, :, cols].bitcast(F32), src).then_inc(loaded[u][c], 16)
                    for row, half in ((0, 0), (HD, 1), (2 * HD, 0)):
                        sp.dma_start(k_st[u][row:row + HD, cols].bitcast(F32),
                                     k_s[half, bass.ds(kv * HD, HD), toks]).then_inc(loaded[u][c], 16)
                    sp.dma_start(v_st[u][:, c * PER:(c + 1) * PER, :],
                                 v_s[toks, bass.ds(kv * HD, HD)].rearrange("(j p) d -> p j d", p=P)
                                 ).then_inc(loaded[u][c], 16)

            load(0, 0)

            def body(g, u, more):
                if more:
                    wait_alone(sp, v_ok, N_V * g + NP, waited)
                    load(g + 1, 1 - u)
                for c in range(CH):
                    batch, kv = g // NKV, g % NKV
                    toks = bass.ds(batch * SEQ + c * BANK, BANK)
                    for half, o, ready in ((0, o_hi, oh_ok), (1, o_lo, ol_ok)):
                        wait_alone(sp, ready, CH * g + c + 1 + 2 * half, waited)
                        sp.dma_start(o_s[half, bass.ds(kv * P, P), toks],
                                     o[:, c % 2, :].bitcast(F32)).then_inc(o_out[c % 2], 16)
            by_groups(sp, body)
            for k in range(2):
                sp.wait_ge(o_out[k], 32 * (GROUPS * CH // 2 + 1))

        @block.gpsimd
        def _(pool):
            pool.memset(ones[:], 1.0).then_inc(set_ok, 1)
            pool.wait_ge(set_ok, 1)
            pool.memset(stage[:].bitcast(F32), 0.0).then_inc(set_ok, 1)
            for u in range(2):
                pool.wait_ge(set_ok, 2 + u)
                pool.memset(k_st[u][MROW:KROWS, :].bitcast(F32), 1.0).then_inc(set_ok, 1)
            for k in range(2):
                pool.sem_inc(o_out[k], 32)
            pool.sem_inc(ol_ok, 2)

            def halves(g, c):
                n = CH * g + c
                pool.wait_ge(norm_ok, n + 1)
                wait_alone(pool, o_out[c % 2], 32 * (CH // 2 * g + c // 2 + 1), waited)
                pool.tensor_copy(o_hi[:, c % 2, :], o_n[:, c % 2, :]).then_inc(oh_ok, 1)
                pool.wait_ge(oh_ok, n + 1)
                pool.tensor_tensor(o_lo[:, c % 2, :], o_n[:, c % 2, :], o_hi[:, c % 2, :].bitcast(F32),
                                   ALU.subtract).then_inc(ol_ok, 1)

            def body(g, u, more):
                for t in range(NS):
                    if t in ADDED:
                        c, j = STEPS[t]
                        q0 = max(0, j - PER * c) * P
                        total = probs[:, ADDED[t] % NP, :, q0:BANK]
                        k = len(ADDS) * g + ADDS.index(t)
                        pool.wait_ge(p_ok, probs_of(g, t))
                        if t == ADDED[t] + 1:
                            pool.wait_ge(v_ok, steps_done(g, ADDED[t]))
                        else:
                            pool.wait_ge(add_ok, k)
                        pool.tensor_tensor(total, total, probs[:, t % NP, :, q0:BANK], ALU.add).then_inc(add_ok, 1)
                    if t - 6 in LAST:
                        halves(g, LAST.index(t - 6))
                halves(g, CH - 1)
            by_groups(pool, body)

        @block.scalar
        def _(act):
            act.sem_inc(p_ok, RING)
            act.sem_inc(turn_used, 1)

            def turned(g, u, n, use):
                i = use[1]
                act.wait_ge(sm_ok, N_USES * g + n + 1)
                act.activation(q_st[u][MROW:KROWS, :, i * P:(i + 1) * P],
                               sm[MROW:KROWS, n % RING, :].rearrange("r (h q) -> r h q", h=GQ),
                               ACT.Copy).then_inc(turn_used, 1)

            for n, use in enumerate(ORDER[:HEAD]):
                if use[0] == "turn":
                    turned(0, 0, n, use)

            def exponential(g, t, h):
                c, j = STEPS[t]
                k, q0 = GQ * t + h, max(0, j - PER * c) * P
                act.wait_ge(st_ok, HEADS * g + k + 1)
                if h == 0:
                    act.wait_ge(v_ok, steps_done(g, t - 2 if t >= 2 else t - 3))
                act.activation(probs[:, t % NP, h, q0:BANK], st[:, head_bank(k), q0:BANK], ACT.Exp,
                               scale=SM_SCALE).then_inc(p_ok, 1)

            for h in range(GQ):
                exponential(0, 0, h)

            def body(g, u, more):
                def turns(t, slots):
                    for slot in slots:
                        for nxt, n, use in USES.get((t, slot), []):
                            if use[0] == "turn" and (more or not nxt):
                                turned(g + nxt, (u + nxt) % 2, n, use)
                for t in range(NS):
                    for h in range(GQ):
                        turns(t, [[0], [1], [2, 3], [4, 5]][h])
                        if h == 3 and t in LAST[:-1]:
                            act.wait_ge(v_ok, steps_done(g, t))
                            act.wait_ge(norm_ok, CH * g + LAST.index(t))
                            act.activation(o_raw[:], o_ps[:], ACT.Copy).then_inc(o_left, 1)
                        if t + 1 < NS:
                            exponential(g, t + 1, h)
                        elif more:
                            exponential(g + 1, 0, h)
            by_groups(act, body)

        @block.tensor
        def _(pe):
            pe.sem_inc(v_ok, NP)
            pe.wait_ge(consts_in, 32)
            pe.wait_ge(set_ok, 4)
            pe.wait_ge(cast_ok, 3)

            def use_bank(g, u, n, use):
                at = n % RING
                kind, count = freed(n)
                if kind == "piece":
                    pe.wait_ge(piece_used, 2 * N_PIECES * g + 2 * count + 1)
                else:
                    pe.wait_ge(turn_used, KTILES * g + count + 1)
                if use[0] == "piece":
                    _, i, h, c = use
                    if i % PER == 0 and h == 0 and c == 0:
                        pe.wait_ge(loaded[u][i // PER], 8 * LOADS * (g - u) + 16 * LOADS)
                    diagonal = c == i // PER
                    w = piece_width(use)
                    mm = pe.matmul(sm[:, at, 0:w], q_st[u][0:MROW, h, i * P:(i + 1) * P],
                                   k_st[u][0:MROW, c * BANK:c * BANK + w], start=True, stop=not diagonal)
                    if diagonal:
                        mm = pe.matmul(sm[:, at, w - P:w], identb[:], masks[:, 0, :], start=False, stop=True)
                else:
                    i = use[1]
                    pe.wait_ge(stage_ok, KTILES * g + i + 1)
                    for h in range(GQ):
                        mm = pe.transpose(sm[0:KROWS, at, h * P:(h + 1) * P].bitcast(F32R),
                                          stage[:, i % 2, h, :], identr[:])
                mm.then_inc(sm_ok, 1)

            def logits(g, u, t, h):
                c, j = STEPS[t]
                k, q0 = GQ * t + h, max(0, j - PER * c) * P
                if j == 0 and h == 0:
                    pe.wait_ge(turn_used, KTILES * g + PER * (c + 1) + 1)
                pe.wait_ge(p_ok, HEADS * g + head_freed(k) + RING)
                masked = j >= PER * c
                mm = pe.matmul(st[:, head_bank(k), q0:BANK], k_st[u][0:KROWS, j * P:(j + 1) * P],
                               q_st[u][0:KROWS, h, c * BANK + q0:(c + 1) * BANK], start=True, stop=not masked)
                if masked:
                    mm = pe.matmul(st[:, head_bank(k), q0:q0 + P], identb[:], masks[:, 1, :], start=False, stop=True)
                mm.then_inc(st_ok, 1)

            def weigh(t, out, sta, first, last):
                c, j = STEPS[t]
                q0 = max(0, j - PER * c) * P
                for h in range(GQ):
                    mm = pe.matmul(out[h * HD:(h + 1) * HD, q0:BANK], sta, probs[:, t % NP, h, q0:BANK],
                                   start=first, stop=last)
                return mm

            def sums(g, at):
                for t in SUMMED.get(at, []):
                    c = STEPS[t][0]
                    mine = [x for _, x in SUM_ORDER if STEPS[x][0] == c]
                    if t == mine[0]:
                        pe.wait_ge(sum_left, CH * g + c + 1)
                    into = [k for k, x in enumerate(ADDS) if ADDED[x] == t]
                    if into:
                        pe.wait_ge(add_ok, len(ADDS) * g + into[-1] + 1)
                    mm = weigh(t, sum_ps, ones[:], t == mine[0], t == mine[-1])
                return mm if SUMMED.get(at) else None

            for n, use in enumerate(ORDER[:HEAD]):
                use_bank(0, 0, n, use)
            for h in range(GQ):
                logits(0, 0, 0, h)

            def body(g, u, more):
                def max_pass(t, slot):
                    for nxt, n, use in USES.get((t, slot), []):
                        if more or not nxt:
                            use_bank(g + nxt, (u + nxt) % 2, n, use)
                def next_logits(t, h):
                    if t + 1 < NS:
                        logits(g, u, t + 1, h)
                    elif more:
                        logits(g + 1, 1 - u, 0, h)

                for t, (c, j) in enumerate(STEPS):
                    for h in range(2):
                        max_pass(t, h)
                        next_logits(t, h)
                    max_pass(t, 2)
                    sums(g, t)
                    max_pass(t, 3)
                    next_logits(t, 2)
                    max_pass(t, 4)
                    pe.wait_ge(p_ok, probs_of(g, t))
                    if j == 0:
                        pe.wait_ge(o_left, CH * g + c + 1)
                    weigh(t, o_ps, v_st[u][:, j, :], j == 0, j == PER * (c + 1) - 1).then_inc(v_ok, 1)
                    max_pass(t, 5)
                    next_logits(t, 3)
                sums(g, NS).then_inc(v_ok, 1)
            by_groups(pe, body)

        @block.vector
        def _(dve):
            dve.sem_inc(piece_used, 1)
            dve.sem_inc(o_left, 1)
            dve.sem_inc(sum_left, 1)
            dve.wait_ge(consts_in, 32)
            dve.tensor_copy(identr[:], ident[:]).then_inc(cast_ok, 1)
            dve.tensor_copy(identb[:], ident[:]).then_inc(cast_ok, 1)
            dve.tensor_copy(masks[:], masks_f[:]).then_inc(cast_ok, 1)
            dve.wait_ge(set_ok, 4)

            def max_of(g, i):
                m, at = KTILES * g + i, i % 2
                pieces = ORDER.index(("piece", i, GQ - 1, i // PER))
                pieces = sum(use[0] == "piece" for use in ORDER[:pieces + 1])

                def largest():
                    dve.wait_ge(piece_used, 2 * N_PIECES * g + 2 * pieces + 1)
                    dve.tensor_reduce(neg_max[:, at, :], mx[:, at, :, 0:i // PER + 1], AX.X, ALU.max,
                                      negate=True).then_inc(m_ok, 1)

                def high():
                    dve.wait_ge(m_ok, 2 * m + 1)
                    dve.tensor_copy(stage[:, at, :, MROW], neg_max[:, at, :]).then_inc(m_ok, 1)

                def low():
                    dve.wait_ge(m_ok, 2 * m + 2)
                    dve.tensor_tensor(stage[:, at, :, MROW + 1], neg_max[:, at, :],
                                      stage[:, at, :, MROW].bitcast(F32), ALU.subtract).then_inc(stage_ok, 1)
                return [largest, high, low]

            def take(g, n, use, chain):
                if use[0] == "turn":
                    return
                _, i, h, c = use
                dve.wait_ge(sm_ok, N_USES * g + n + 1)
                w = piece_width(use)
                dve.tensor_reduce(mx[:, i % 2, h, c:c + 1], sm[:, n % RING, 0:w], AX.X, ALU.max).then_inc(piece_used, 2)
                if chain:
                    chain.pop(0)()
                if (h, c) == (GQ - 1, i // PER):
                    chain += max_of(g, i)
                    if i == KTILES - 1:
                        while chain:
                            chain.pop(0)()

            chain = []
            for n, use in enumerate(ORDER[:HEAD]):
                take(0, n, use, chain)
            assert not chain

            def normalise(g, c):
                n = CH * g + c
                blocks = sum_t[:].rearrange("p (b k) -> p b k", k=HD)

                def turn():
                    dve.wait_ge(v_ok, N_V * (g + 1) + NP if c == CH - 1 else steps_done(g, LAST[c] + 2))
                    dve.transpose(sum_t[:], sum_ps[:]).then_inc(sum_left, 1)

                def invert():
                    dve.wait_ge(sum_left, n + 2)
                    dve.reciprocal(recip_t[:], blocks[:, :, 0]).then_inc(recip_ok, 1)

                def turn_back():
                    dve.wait_ge(recip_ok, 2 * n + 1)
                    dve.transpose(recip[:].rearrange("p (b k) -> p b k", k=HD),
                                  recip_t[:].unsqueeze(2).broadcast_to([P, BANK // HD, HD])).then_inc(recip_ok, 1)

                def scale():
                    dve.wait_ge(recip_ok, 2 * n + 2)
                    dve.wait_ge(o_left, n + 2)
                    dve.wait_ge(ol_ok, n + 1)
                    dve.tensor_tensor(o_n[:, c % 2, :], o_raw[:], recip[:], ALU.mult).then_inc(norm_ok, 1)
                return [turn, invert, turn_back, scale]

            def body(g, u, more):
                chain = []
                for t in range(NS):
                    if t - 3 in LAST:
                        norm = normalise(g, LAST.index(t - 3))
                    for slot in range(SLOTS):
                        if t - 3 in LAST and norm:
                            norm.pop(0)()
                        for nxt, n, use in USES.get((t, slot), []):
                            if more or not nxt:
                                take(g + nxt, n, use, chain)
                assert not chain
                dve.wait_ge(v_ok, steps_done(g, NS - 1))
                dve.wait_ge(norm_ok, CH * g + CH - 1)
                dve.tensor_copy(o_raw[:], o_ps[:]).then_inc(o_left, 1)
                for part in normalise(g, CH - 1):
                    part()
            by_groups(dve, body)


def output(nc, x, wo, wb, bias, w_router, lora_a, lora_b, ident_d, iota_d, o_s, out):
    with ExitStack() as ctx:
        s = Scope(nc, ctx, "p3")
        ident = s.sb("ident", [P, P], F32)
        iota = s.sb("iota", [P, EXPERTS], F32)
        bias_t = s.sb("bias", [P, HID], F32)
        wo_hi = s.sb("wo_hi", [P, KT, HID], F32R)
        wo_lo = s.sb("wo_lo", [P, KT, HID], F32R)
        wb_hi = s.sb("wb_hi", [P, KT, HID + ARW], F32R)
        wb_lo = s.sb("wb_lo", [P, KT, HID + ARW], F32R)
        b_hi = s.sb("b_hi", [P, HID], F32R)
        b_lo = s.sb("b_lo", [P, HID], F32R)
        x_t = s.sb("x", [P, 2, HID], F32)
        res = s.sb("res", [P, 2, HID], F32)
        bn = s.sb("bn", [P, 2, HID // BANK, 6], F32)
        mean_var = s.sb("mean_var", [P, 2, 2], F32)
        var_eps = s.sb("var_eps", [P, 2], F32)
        rstd = s.sb("rstd", [P, 2], F32)
        minus_half = s.sb("minus_half", [P, 1], F32)
        xt_hi = s.sb("xt_hi", [P, 2, KT, P], F32R)
        xt_lo = s.sb("xt_lo", [P, 2, KT, P], F32R)
        o_hi = s.sb("o_hi", [P, 2, KT, P], F32R)
        o_lo = s.sb("o_lo", [P, 2, KT, P], F32R)
        ar = s.sb("ar", [P, ARW], F32)
        top = s.sb("top", [P, 8], F32)
        at = s.sb("at", [P, 8], U32)
        at_f = s.sb("at_f", [P, 2], F32)
        gap = s.sb("gap", [P, 1], F32)
        e_gap = s.sb("e_gap", [P, 1], F32)
        half_sum = s.sb("half_sum", [P, 1], F32)
        w_top = s.sb("w_top", [P, 2], F32)
        gate = s.sb("gate", [P, 2, EXPERTS], F32)
        gates = s.sb("gates", [P, EXPERTS], F32)
        hg = s.sb("hg", [P, ADW], F32)
        hgt_hi = s.sb("hgt_hi", [P, P], F32R)
        hgt_lo = s.sb("hgt_lo", [P, P], F32R)
        tp = s.ps("tp", [P, KT * P])
        acc = s.ps("acc", [P, 2, 3, BANK])

        consts_in = s.sem("consts_in")
        waited = s.sem("waited")
        nat = [x_t[:, 0, :], x_t[:, 1, :], res[:, 0, :]]
        b_nat = res[:, 1, :]
        NAT = len(nat)
        w_in = [s.sem(f"w_in{k}") for k in range(NAT)]
        b_in = s.sem("b_in")
        w_tp = s.sem("w_tp")
        w_hi_ok = s.sem("w_hi_ok")
        w_lo_ok = s.sem("w_lo_ok")
        x_in = [s.sem("x_in0"), s.sem("x_in1")]
        o_in = [s.sem("o_in0"), s.sem("o_in1")]
        bn_ok = s.sem("bn_ok")
        var_ok = s.sem("var_ok")
        eps_ok = s.sem("eps_ok")
        rstd_ok = s.sem("rstd_ok")
        res_ok = s.sem("res_ok")
        xn_ok = s.sem("xn_ok")
        tp_ok = s.sem("tp_ok")
        xh_ok = s.sem("xh_ok")
        xl_ok = s.sem("xl_ok")
        ar_ok = s.sem("ar_ok")
        ar_left = s.sem("ar_left")
        gap_ok = s.sem("gap_ok")
        e_ok = s.sem("e_ok")
        gate_ok = s.sem("gate_ok")
        hg_ok = s.sem("hg_ok")
        ht_ok = s.sem("ht_ok")
        hgt_ok = s.sem("hgt_ok")
        hgl_ok = s.sem("hgl_ok")
        acc_ok = s.sem("acc_ok")
        out_ok = s.sem("out_ok")
        out_in = [s.sem("out_in0"), s.sem("out_in1")]
        mh_ok = s.sem("mh_ok")
        GATE_STEPS = 7

        weights = []
        for w, hi, lo in ((wo, wo_hi, wo_lo), (wb, wb_hi, wb_lo)):
            for r in range(KT):
                at_col = r * P + (ARW if w is wb and r * P >= FIRST else 0)
                weights.append((w[r * P:(r + 1) * P, :], P, hi[:, :, at_col:at_col + P], lo[:, :, at_col:at_col + P]))
        for w, rows, at_col in ((lora_a.rearrange("e r d -> (e r) d"), P, FIRST), (w_router, EXPERTS, FIRST + ADW)):
            weights.append((w, rows, wb_hi[:, :, at_col:at_col + rows], wb_lo[:, :, at_col:at_col + rows]))
        NW = len(weights)
        w_ps = [tp[:]] + [acc[:, u, 0:2, :].rearrange("p b c -> p (b c)") for u in range(2)]
        WPS = len(w_ps)
        columns = [slice(0, FIRST), slice(FIRST, FIRST + REST), slice(FIRST + REST, HID)]

        block = ctx.enter_context(nc.Block())

        @block.sync
        def _(sp):
            sp.dma_start(ident[:], ident_d).then_inc(consts_in, 16)
            sp.dma_start(iota[:], iota_d).then_inc(consts_in, 16)
            sp.dma_start(bias_t[:], bias.partition_broadcast(P)).then_inc(consts_in, 16)
            for n, (w, rows, _, _) in enumerate(weights):
                if n >= NAT:
                    sp.wait_ge(w_tp, n - NAT + 1)
                sp.dma_start(nat[n % NAT][0:rows, :], w).then_inc(w_in[n % NAT], 16)

            def load_x(n, u):
                if before(n, 2):
                    sp.wait_ge(w_tp, max(range(n, NW, NAT)) + 1)
                else:
                    wait_alone(sp, tp_ok, n - 1, waited)
                sp.dma_start(x_t[:, u, :], x[bass.ds(n * P, P), :]).then_inc(x_in[u], 16)

            def load_o(n, u):
                if not before(n, 2):
                    wait_alone(sp, acc_ok, n - 1, waited)
                for half, o in ((0, o_hi), (1, o_lo)):
                    sp.dma_start(o[:, u].bitcast(F32),
                                 o_s[half, :, bass.ds(n * P, P)].rearrange("(k p) t -> p k t", p=P)
                                 ).then_inc(o_in[u], 16)

            def store(n, u):
                wait_alone(sp, out_ok, n + 1, waited)
                sp.dma_start(out[bass.ds(n * P, P), :], res[:, u, :]).then_inc(out_in[u], 16)
            for n in range(2):
                load_x(n, n)
                load_o(n, n)
            by_pairs(sp, TILES - 2, lambda n, u: (load_x(n + 2, u), load_o(n + 2, u), store(n, u)))
            store(TILES - 2, 0)
            store(TILES - 1, 1)
            for u in range(2):
                sp.wait_ge(out_in[u], 16 * TILES // 2)

        @block.gpsimd
        def _(pool):
            pool.memset(minus_half[:], -0.5).then_inc(mh_ok, 1)
            pool.wait_ge(mh_ok, 1)
            pool.wait_ge(consts_in, 48)

            def tile(n, u):
                pool.wait_ge(x_in[u], 8 * (n - u) + 16)
                if before(n, 2):
                    pool.wait_ge(w_tp, NW + n)
                else:
                    pool.wait_ge(out_in[u], 8 * (n - u))
                pool.tensor_tensor(res[:, u, :], x_t[:, u, :], bias_t[:], ALU.add).then_inc(res_ok, 1)
                wait_alone(pool, var_ok, n + 1, waited)
                pool.tensor_scalar(var_eps[:, u:u + 1], mean_var[:, u, 1:2], EPS, None, ALU.add).then_inc(eps_ok, 1)
                pool.wait_ge(eps_ok, n + 1)
                pool.tensor_tensor(rstd[:, u:u + 1], var_eps[:, u:u + 1], minus_half[:], ALU.pow).then_inc(rstd_ok, 1)
            by_pairs(pool, TILES, tile)

        @block.scalar
        def _(act):
            for k in range(KT):
                act.dma_start(b_nat[:, k * P:(k + 1) * P].rearrange("p (e r) -> p e r", e=EXPERTS),
                              lora_b[:, k * P:(k + 1) * P, :].rearrange("e o r -> o e r")).then_inc(b_in, 16)
            for n, (_, _, hi, _) in enumerate(weights):
                act.wait_ge(w_tp, n + 1)
                cols = hi.shape[2]
                act.activation(hi, w_ps[n % WPS][:, 0:KT * cols].rearrange("p (k c) -> p k c", k=KT),
                               ACT.Copy).then_inc(w_hi_ok, 1)
            act.wait_ge(w_tp, NW + 1)
            act.activation(b_hi[:], tp[:], ACT.Copy).then_inc(w_hi_ok, 1)

            def x_hi(n, u):
                act.wait_ge(tp_ok, n + 1)
                if not before(n, 2):
                    act.wait_ge(acc_ok, n - 1)
                act.activation(xt_hi[:, u].rearrange("p k c -> p (k c)"), tp[:], ACT.Copy).then_inc(xh_ok, 1)

            x_hi(0, 0)

            def tile(n, u):
                act.wait_ge(gap_ok, n + 1)
                act.activation(e_gap[:], gap[:], ACT.Exp).then_inc(e_ok, 1)
                if not (isinstance(n, int) and n == TILES - 1):
                    x_hi(n + 1, 1 - u)
                act.wait_ge(ht_ok, n + 1)
                if not before(n, 1):
                    act.wait_ge(acc_ok, n)
                act.activation(hgt_hi[:], tp[:, 0:P], ACT.Copy).then_inc(hgt_ok, 1)
            by_pairs(act, TILES, tile)

        @block.tensor
        def _(pe):
            pe.wait_ge(consts_in, 48)
            for n, (_, rows, hi, _) in enumerate(weights):
                pe.wait_ge(w_in[n % NAT], 16 * (n // NAT + 1))
                if n >= WPS:
                    pe.wait_ge(w_hi_ok, n - WPS + 1)
                    pe.wait_ge(w_lo_ok, n - WPS + 1)
                for k in range(KT):
                    mm = pe.transpose(w_ps[n % WPS][:, k * rows:(k + 1) * rows], nat[n % NAT][0:rows, k * P:(k + 1) * P],
                                      ident[0:rows, 0:rows])
                mm.then_inc(w_tp, 1)
            pe.wait_ge(b_in, 16 * KT)
            pe.wait_ge(w_hi_ok, NW)
            pe.wait_ge(w_lo_ok, NW)
            for k in range(KT):
                mm = pe.transpose(tp[:, k * P:(k + 1) * P], b_nat[:, k * P:(k + 1) * P], ident[:])
            mm.then_inc(w_tp, 1)

            def turn_x(n, u):
                pe.wait_ge(xn_ok, n + 1)
                if before(n, 1):
                    pe.wait_ge(w_hi_ok, NW + 1)
                    pe.wait_ge(w_lo_ok, NW + 1)
                else:
                    pe.wait_ge(xh_ok, n)
                    pe.wait_ge(xl_ok, n)
                    if not before(n, 2):
                        pe.wait_ge(hgl_ok, n - 1)
                for k in range(KT):
                    mm = pe.transpose(tp[:, k * P:(k + 1) * P], x_t[:, u, k * P:(k + 1) * P], ident[:])
                mm.then_inc(tp_ok, 1)

            def base_products(u, b):
                width = FIRST + ARW if b == 0 else REST
                col = 0 if b == 0 else columns[b].start + ARW
                for k in range(KT):
                    mm = three_passes(pe, acc[:, u, b, 0:width], xt_hi[:, u, k, :], xt_lo[:, u, k, :],
                                      wb_hi[:, k, col:col + width], wb_lo[:, k, col:col + width],
                                      k == 0, b == 0 and k == KT - 1)
                return mm

            def o_products(u, b):
                cols = columns[b]
                for k in range(KT):
                    three_passes(pe, acc[:, u, b, 0:cols.stop - cols.start], o_hi[:, u, k, :], o_lo[:, u, k, :],
                                 wo_hi[:, k, cols], wo_lo[:, k, cols], b == 0 and k == 0, False)

            turn_x(0, 0)

            def tile(n, u):
                pe.wait_ge(xh_ok, n + 1)
                pe.wait_ge(xl_ok, n + 1)
                if not before(n, 2):
                    pe.wait_ge(out_ok, n - 1)
                base_products(u, 0).then_inc(ar_ok, 1)
                base_products(u, 1)
                pe.wait_ge(o_in[u], 16 * (n - u) + 32)
                o_products(u, 1)
                last = isinstance(n, int) and n == TILES - 1
                if not last:
                    turn_x(n + 1, 1 - u)
                base_products(u, 2)
                o_products(u, 2)
                pe.wait_ge(hg_ok, n + 1)
                if not last:
                    pe.wait_ge(xh_ok, n + 2)
                    pe.wait_ge(xl_ok, n + 2)
                pe.transpose(tp[:, 0:P], hg[:], ident[:]).then_inc(ht_ok, 1)
                pe.wait_ge(ar_left, n + 1)
                o_products(u, 0)
                pe.wait_ge(hgt_ok, n + 1)
                pe.wait_ge(hgl_ok, n + 1)
                for b, cols in enumerate(columns):
                    mm = three_passes(pe, acc[:, u, b, 0:cols.stop - cols.start], hgt_hi[:], hgt_lo[:],
                                      b_hi[:, cols], b_lo[:, cols], False, True)
                mm.then_inc(acc_ok, 1)
            by_pairs(pe, TILES, tile)

        @block.vector
        def _(dve):
            dve.wait_ge(consts_in, 48)
            for n, (_, _, hi, lo) in enumerate(weights):
                cols = hi.shape[2]
                dve.wait_ge(w_hi_ok, n + 1)
                dve.tensor_tensor(lo, w_ps[n % WPS][:, 0:KT * cols].rearrange("p (k c) -> p k c", k=KT),
                                  hi.bitcast(F32), ALU.subtract).then_inc(w_lo_ok, 1)

            def normalise(n, u):
                dve.wait_ge(x_in[u], 8 * (n - u) + 16)
                for c in range(HID // BANK):
                    dve.bn_stats(bn[:, u, c, :], x_t[:, u, c * BANK:(c + 1) * BANK]).then_inc(bn_ok, 1)
                wait_alone(dve, bn_ok, 2 * n + 2, waited)
                dve.bn_aggr(mean_var[:, u, :], bn[:, u].rearrange("p c s -> p (c s)")).then_inc(var_ok, 1)
                dve.wait_ge(var_ok, n + 1)
                dve.wait_ge(rstd_ok, n + 1)
                dve.wait_ge(res_ok, n + 1)
                dve.tensor_scalar(x_t[:, u, :], x_t[:, u, :], mean_var[:, u, 0:1], rstd[:, u:u + 1],
                                  ALU.subtract, ALU.mult).then_inc(xn_ok, 1)

            def x_lo(n, u):
                dve.wait_ge(xh_ok, n + 1)
                dve.tensor_tensor(xt_lo[:, u].rearrange("p k c -> p (k c)"), tp[:],
                                  xt_hi[:, u].rearrange("p k c -> p (k c)").bitcast(F32),
                                  ALU.subtract).then_inc(xl_ok, 1)

            def route(n, u):
                step = 0

                def then(ins):
                    nonlocal step
                    step += 1
                    ins.then_inc(gate_ok, 1)
                    wait_alone(dve, gate_ok, GATE_STEPS * n + step, waited)
                dve.wait_ge(ar_ok, n + 1)
                dve.tensor_copy(ar[:], acc[:, u, 0, FIRST:FIRST + ARW])
                first = res[:, u, 0:FIRST]
                dve.tensor_tensor(first, acc[:, u, 0, 0:FIRST], first, ALU.add).then_inc(ar_left, 1)
                wait_alone(dve, ar_left, n + 1, waited)
                logit = ar[:, ADW:ARW]
                then(dve.max(out=top[:], in_=logit))
                dve.tensor_tensor(gap[:], top[:, 1:2], top[:, 0:1], ALU.subtract).then_inc(gap_ok, 1)
                then(dve.max_index(out=at[:], in_max=top[:], in_values=logit))
                dve.tensor_copy(at_f[:], at[:, 0:2])
                dve.wait_ge(e_ok, n + 1)
                then(dve.tensor_scalar(half_sum[:], e_gap[:], 1.0, 1.0 / LORA_SCALE, ALU.add, ALU.mult))
                then(dve.reciprocal(w_top[:, 0:1], half_sum[:]))
                then(dve.tensor_tensor(w_top[:, 1:2], w_top[:, 0:1], e_gap[:], ALU.mult))
                for k in range(2):
                    ins = dve.tensor_scalar(gate[:, k, :], iota[:], at_f[:, k:k + 1], w_top[:, k:k + 1],
                                            ALU.is_equal, ALU.mult)
                then(ins)
                then(dve.tensor_tensor(gates[:], gate[:, 0, :], gate[:, 1, :], ALU.add))
                dve.tensor_tensor(hg[:].rearrange("p (e r) -> p e r", e=EXPERTS),
                                  ar[:, 0:ADW].rearrange("p (e r) -> p e r", e=EXPERTS),
                                  gates[:].unsqueeze(2).broadcast_to([P, EXPERTS, RANK]),
                                  ALU.mult).then_inc(hg_ok, 1)
                assert step == GATE_STEPS

            def finish(n, u):
                dve.wait_ge(acc_ok, n + 1)
                first = res[:, u, 0:FIRST]
                rest = res[:, u, FIRST:HID].rearrange("p (b c) -> p b c", c=REST)
                dve.tensor_tensor(first, acc[:, u, 0, 0:FIRST], first, ALU.add)
                dve.tensor_tensor(rest, acc[:, u, 1:3, 0:REST], rest, ALU.add).then_inc(out_ok, 1)

            normalise(0, 0)
            dve.wait_ge(w_hi_ok, NW + 1)
            dve.tensor_tensor(b_lo[:], tp[:], b_hi[:].bitcast(F32), ALU.subtract).then_inc(w_lo_ok, 1)
            x_lo(0, 0)

            def tile(n, u):
                if not before(n, 1):
                    finish(n - 1, 1 - u)
                last = isinstance(n, int) and n == TILES - 1
                if not last:
                    normalise(n + 1, 1 - u)
                route(n, u)
                if not last:
                    x_lo(n + 1, 1 - u)
                dve.wait_ge(hgt_ok, n + 1)
                dve.tensor_tensor(hgt_lo[:], tp[:, 0:P], hgt_hi[:].bitcast(F32), ALU.subtract).then_inc(hgl_ok, 1)
            by_pairs(dve, TILES, tile)
            finish(TILES - 1, 1)


def build(nc, ins, out):
    def scratch(name, shape):
        return nc.dram_tensor(name, shape, F32, kind="Internal").ap()
    q_s = scratch("q_halves", [2, HID, TOKENS])
    k_s = scratch("k_halves", [2, KVW, TOKENS])
    v_s = scratch("v_rows", [TOKENS, KVW])
    o_s = scratch("o_halves", [2, HID, TOKENS])
    x = ins["L0_attn_hidden_states"].rearrange("b s d -> (b s) d")
    project_qkv(nc, x, ins["L0_attn_Wq"], ins["L0_attn_Wk"], ins["L0_attn_Wv"], ins["rope"], ins["ident"],
                q_s, k_s, v_s)
    attention(nc, q_s, k_s, v_s, ins["ident"], ins["masks"], o_s)
    output(nc, x, ins["L0_attn_Wo"], ins["L0_ffn_W_base"], ins["L0_ffn_b_base"], ins["L0_ffn_W_router"],
           ins["L0_ffn_lora_A"], ins["L0_ffn_lora_B"], ins["ident"], ins["iota"], o_s,
           out.rearrange("b s d -> (b s) d"))


def constants():
    import numpy as np

    inv_freq = (1.0 / np.float32(10000.0) ** (np.arange(0, HD, 2, dtype=np.float32) / np.float32(HD))).astype(np.float32)
    angle = np.outer(np.arange(SEQ, dtype=np.float32), inv_freq).astype(np.float32)
    cos, sin = np.cos(angle), np.sin(angle)
    row = np.concatenate([cos, cos, -sin, sin], axis=1).astype(np.float32)
    order = np.arange(P)
    hidden = np.where(order[None, :] <= order[:, None], 0.0, -1e30)
    return {
        "rope": np.ascontiguousarray(np.tile(row, (BATCH, 1)).reshape(TILES, P, 2 * HD).transpose(1, 0, 2)),
        "ident": np.eye(P, dtype=np.float32),
        "masks": np.stack([hidden, hidden.T], axis=1).astype(np.float32),
        "iota": np.tile(np.arange(EXPERTS, dtype=np.float32), (P, 1)),
    }


def kernel(**inputs):
    import numpy as np
    import concourse.bacc as bacc
    from concourse.bass_utils import run_bass_kernel_spmd

    nc = bacc.Bacc("TRN2", target_bir_lowering=False, num_devices=1)
    arrays, ins = {}, {}
    for name, value in {**inputs, **constants()}.items():
        a = np.ascontiguousarray(value)
        arrays[f"in_{name}"] = a
        ins[name] = nc.dram_tensor(f"in_{name}", a.shape, mybir.dt.from_np(a.dtype), kind="ExternalInput").ap()
    out = nc.dram_tensor("out_dram", (BATCH, SEQ, HID), F32, kind="ExternalOutput").ap()
    build(nc, ins, out)
    r = run_bass_kernel_spmd(nc, [arrays], core_ids=[0])
    return r.results[0]["out_dram"]
```
